# Optimizing a Trainium2 kernel written in Bass

```python
import numpy as np
import jax
import jax.numpy as jnp

def _softmax(x, axis=-1):
    return jax.nn.softmax(x, axis=axis)

def _gelu(x):
    return jax.nn.gelu(x, approximate=True)

def _silu(x):
    return jax.nn.silu(x)

def _sigmoid(x):
    return jax.nn.sigmoid(x)

def _layernorm(x, axis=-1, eps=1e-05):
    m = jnp.mean(x, axis=axis, keepdims=True)
    v = jnp.var(x, axis=axis, keepdims=True)
    return (x - m) / jnp.sqrt(v + eps)

def _scatter_add(tgt, idx, src, axis=0):
    return tgt.at[idx].add(src)

def _segment_sum(src, seg, n):
    return jax.ops.segment_sum(src, seg, n)
kernel_name = 'mk_prb_d1_jaxref_r8_855086'

def setup_inputs(seed: int=0):
    np.random.seed(seed)
    _w = jnp.asarray

    def _L0_attn_setup():
        import jax, jax.numpy as jnp
        import numpy as np
        DIM = 128
        NUM_HEADS = 16
        key = jax.random.key(seed)
        k_x, k_qw, k_qb, k_pw, k_pb = jax.random.split(key, 5)
        x = jax.random.normal(k_x, (2, 256, DIM), dtype=jnp.float32)
        s = 1.0 / np.sqrt(DIM)
        qkv_w = jax.random.uniform(k_qw, (3 * DIM, DIM), minval=-s, maxval=s, dtype=jnp.float32)
        qkv_b = jax.random.uniform(k_qb, (3 * DIM,), minval=-s, maxval=s, dtype=jnp.float32)
        proj_w = jax.random.uniform(k_pw, (DIM, DIM), minval=-s, maxval=s, dtype=jnp.float32)
        proj_b = jax.random.uniform(k_pb, (DIM,), minval=-s, maxval=s, dtype=jnp.float32)
        return {'x': x, 'qkv_w': qkv_w, 'qkv_b': qkv_b, 'proj_w': proj_w, 'proj_b': proj_b}
    _L0_attn_in = _L0_attn_setup()

    def _L0_ffn_setup():
        import jax, jax.numpy as jnp
        import numpy as np
        B, T, D, H, E, TOPK = (2, 256, 128, 512, 8, 2)

        def sq_relu(x):
            return jnp.square(jax.nn.relu(x))
        key = jax.random.key(seed)
        ks = jax.random.split(key, 6)
        s = 0.02
        return {'x': jax.random.normal(ks[0], (B, T, D), dtype=jnp.float32), 'W_router': jax.random.normal(ks[1], (D, E), dtype=jnp.float32) * s, 'W_up': jax.random.normal(ks[2], (E, D, H), dtype=jnp.float32) * s, 'W_down': jax.random.normal(ks[3], (E, H, D), dtype=jnp.float32) * s, 'W_sh_up': jax.random.normal(ks[4], (D, H), dtype=jnp.float32) * s, 'W_sh_down': jax.random.normal(ks[5], (H, D), dtype=jnp.float32) * s}
    _L0_ffn_in = _L0_ffn_setup()
    _d = {'L0_attn_x': _L0_attn_in['x'], 'L0_attn_qkv_w': _L0_attn_in['qkv_w'], 'L0_attn_qkv_b': _L0_attn_in['qkv_b'], 'L0_attn_proj_w': _L0_attn_in['proj_w'], 'L0_attn_proj_b': _L0_attn_in['proj_b'], 'L0_ffn_W_router': _L0_ffn_in['W_router'], 'L0_ffn_W_up': _L0_ffn_in['W_up'], 'L0_ffn_W_down': _L0_ffn_in['W_down'], 'L0_ffn_W_sh_up': _L0_ffn_in['W_sh_up'], 'L0_ffn_W_sh_down': _L0_ffn_in['W_sh_down']}
    _x0 = _d['L0_attn_x']
    _d['L0_attn_x'] = jax.random.normal(jax.random.fold_in(jax.random.key(seed), 1), (16, 256, 128), dtype=_x0.dtype)
    del _x0
    return _d

def reference(L0_attn_x, L0_attn_qkv_w, L0_attn_qkv_b, L0_attn_proj_w, L0_attn_proj_b, L0_ffn_W_router, L0_ffn_W_up, L0_ffn_W_down, L0_ffn_W_sh_up, L0_ffn_W_sh_down):

    def _L0_attn_ref(x, qkv_w, qkv_b, proj_w, proj_b):
        import jax, jax.numpy as jnp
        import numpy as np
        DIM = 128
        NUM_HEADS = 16
        B, N, C = x.shape
        H = NUM_HEADS
        D = C // H
        qkv = x @ qkv_w.T + qkv_b
        qkv = qkv.reshape(B, N, 3, H, D)
        q, k, v = (qkv[:, :, i].transpose(0, 2, 1, 3) for i in range(3))
        scale = D ** (-0.5)
        attn = jnp.einsum('bhnd,bhmd->bhnm', q, k) * scale
        attn = jax.nn.softmax(attn, axis=-1)
        out = jnp.einsum('bhnm,bhmd->bhnd', attn, v)
        out = out.transpose(0, 2, 1, 3).reshape(B, N, C)
        return out @ proj_w.T + proj_b

    def _L0_ffn_ref(x, W_router, W_up, W_down, W_sh_up, W_sh_down):
        import jax, jax.numpy as jnp
        import numpy as np
        B, T, D, H, E, TOPK = (2, 256, 128, 512, 8, 2)

        def sq_relu(x):
            return jnp.square(jax.nn.relu(x))
        Bb, Tt, Dd = x.shape
        x_flat = x.reshape(-1, Dd)
        N = x_flat.shape[0]
        logits = x_flat @ W_router
        probs = jax.nn.sigmoid(logits)
        topk_probs, topk_idx = jax.lax.top_k(probs, TOPK)
        topk_probs = topk_probs / (jnp.sum(topk_probs, axis=-1, keepdims=True) + 1e-06)
        combine = jnp.zeros((N, E), dtype=x.dtype).at[jnp.arange(N)[:, None], topk_idx].add(topk_probs)
        out = sq_relu(x_flat @ W_sh_up) @ W_sh_down
        for e in range(E):
            h = sq_relu(x_flat @ W_up[e])
            out = out + combine[:, e:e + 1] * (h @ W_down[e])
        return out.reshape(Bb, Tt, Dd)
    x = L0_attn_x
    xn = _layernorm(x, axis=-1)
    x = x + _L0_attn_ref(xn, L0_attn_qkv_w, L0_attn_qkv_b, L0_attn_proj_w, L0_attn_proj_b) + _L0_ffn_ref(xn, L0_ffn_W_router, L0_ffn_W_up, L0_ffn_W_down, L0_ffn_W_sh_up, L0_ffn_W_sh_down)
    return x

_drawn_inputs = setup_inputs


def setup_inputs(seed=0):
    import zlib

    import numpy as np

    out = dict(_drawn_inputs(seed))
    spreads = {}
    factors = {'L0_ffn_W_router': 3.229, 'L0_ffn_W_up': 3.105, 'L0_ffn_W_down': 2.84}
    for name, (base, spread) in spreads.items():
        noise = np.random.default_rng([zlib.crc32(name.encode()), seed]).standard_normal(out[name].shape)
        drawn = base * np.exp(spread * noise) if base else spread * noise
        out[name] = jnp.asarray(drawn.astype(out[name].dtype))
    for name, factor in factors.items():
        out[name] = (out[name] * factor).astype(out[name].dtype)
    return out
```

```python
from contextlib import ExitStack

import concourse.bass as bass
from concourse import mybir

F32 = mybir.dt.float32
F32R = mybir.dt.float32r
ALU = mybir.AluOpType
ACT = mybir.ActivationFunctionType
AX_X = mybir.AxisListType.X

P = 128
B, T, D = 16, 256, 128
NH, HD = 16, 8
GROUPS, LANES = 4, 4
TT = T // P
TILES = B * TT
E, H = 8, 512
HC = H // P
FFNS = E + 1
SCALE = HD ** -0.5
EPS = 1e-5
SLOTS = 8
CHUNK = 4
PART = [8, 16, 24]
QLO, KLO = 1, 2

NU = 16
NC = FFNS * HC
NE = FFNS


def filler():
    items = []
    for e in range(FFNS):
        for c in range(HC):
            items.append(("up", e, c))
            if e and c == 1:
                items.append(("down", e - 1, 0))
    items.append(("down", FFNS - 1, 0))
    n = 2 * SLOTS
    return [items[len(items) * k // n:len(items) * (k + 1) // n] for k in range(n)]


FILL = filler()
CHUNK_OF = {(e, c): e * HC + c for e in range(FFNS) for c in range(HC)}


def build(nc, x, wqkvT, bqkv, wprojT, bproj, w_router, w_up, w_down, w_sup, w_sdown, out):
    with ExitStack() as ctx:
        def sb(name, shape, dt=F32):
            return ctx.enter_context(nc.sbuf_tensor(name, shape, dt))

        def bank(name):
            return ctx.enter_context(nc.psum_tensor(name, [P, 512], F32))

        def sem(name):
            return ctx.enter_context(nc.semaphore(name))

        X = sb("X", [P, TILES, D])
        xTh = sb("xTh", [P, B * T], F32R)
        xTl = sb("xTl", [P, B * T], F32R)
        Uh = sb("Uh", [P, FFNS, H], F32R)
        Ul = sb("Ul", [P, FFNS, H], F32R)
        Dn = sb("Dn", [P, FFNS, HC, D])
        Wqh = sb("Wqh", [P, 2, GROUPS, P], F32R)
        Wql = sb("Wql", [P, 2, GROUPS, P], F32R)
        wst = sb("wst", [P, 3 * D])
        wsh = sb("wsh", [P, 3 * D], F32R)
        wsl = sb("wsl", [P, 3 * D], F32R)
        Wp = sb("Wp", [P, D])
        Wr = sb("Wr", [P, E])
        ident = sb("ident", [P, P])
        bias = sb("bias", [P, 20])
        BVP = sb("BVP", [P, 2 * D])
        st6 = sb("st6", [P, TILES, 6])
        mv = sb("mv", [P, TILES, 2])
        nrm = sb("nrm", [P, 4, TILES])
        pr = sb("pr", [P, TILES, E])
        comb = sb("comb", [P, TILES, E])
        rm = sb("rm", [P, 4, TILES])
        wte = sb("wte", [P, E])
        xch = sb("xch", [P, 2, T], F32R)
        xcl = sb("xcl", [P, 2, T], F32R)
        ccur = sb("ccur", [P, 2, TT * E])
        Qd = sb("Qd", [P, GROUPS, T], F32R)
        tmp = sb("tmp", [P, 2, 2, T], F32R)
        Kd = sb("Kd", [P, 2, GROUPS, T], F32R)
        Qb = sb("Qb", [P, 2, GROUPS, LANES, T], F32R)
        V = sb("V", [P, 2, TT, NH, 32])
        PT = sb("PT", [P, 4, 512])
        Mx = sb("Mx", [P, 2, TT, LANES, 2])
        NM = sb("NM", [8, 2, T], F32R)
        OS = sb("OS", [P, 2, 2, T])
        rs = sb("rs", [P, 2, 2 * TT * LANES])
        AN = sb("AN", [P, TT, D])
        AT = sb("AT", [P, T])
        R = sb("R", [P, 2, T])
        hT = sb("hT", [P, 2, HC, T])

        rows = PT[0:1].rearrange("p a b -> p (a b)")
        rt = PT[:].rearrange("p a b -> p (a b)").rearrange("p (k t e) -> p k t e", t=TILES, e=E)
        ust = OS[:].rearrange("p a b c -> p a (b c)")
        xn = hT[:, 0].rearrange("p a b -> p (a b)").rearrange("p (r t d) -> p r t d", r=2, t=CHUNK)
        xf = hT[:, 1].rearrange("p a b -> p (a b)").rearrange("p (r t) -> p r t", r=2)

        sbank = [bank("sbank0"), bank("sbank1")]
        tbank = [bank("tbank0"), bank("tbank1")]
        obank = bank("obank")
        misc = bank("misc")
        ubank = bank("ubank")
        ybank = bank("ybank")

        s_x = [sem(f"s_x{c}") for c in range(4)]
        s_w = sem("s_w")
        s_u = [sem("s_u0"), sem("s_u1")]
        s_uh = sem("s_uh")
        s_ul = sem("s_ul")
        s_dn = sem("s_dn")
        s_id = sem("s_id")
        s_set = sem("s_set")
        s_wsh = sem("s_wsh")
        s_rows = sem("s_rows")
        s_bps = sem("s_bps")
        s_bias = sem("s_bias")
        s_stat = sem("s_stat")
        s_sq = sem("s_sq")
        s_xn = sem("s_xn")
        s_xnT = sem("s_xnT")
        s_xf = sem("s_xf")
        s_lo = sem("s_lo")
        s_hi = sem("s_hi")
        s_lg = sem("s_lg")
        s_pe_ = sem("s_pe_")
        s_comb = sem("s_comb")
        s_xb = sem("s_xb")
        s_dve = sem("s_dve")
        s_xc = sem("s_xc")
        s_st = sem("s_st")
        s_s = sem("s_s")
        s_pv = sem("s_pv")
        s_tr = sem("s_tr")
        s_ant = sem("s_ant")
        s_y = sem("s_y")
        s_mt = sem("s_mt")
        s_p01 = sem("s_p01")
        s_p23 = sem("s_p23")
        s_vps = sem("s_vps")
        s_e = sem("s_e")
        s_t01 = sem("s_t01")
        s_t23 = sem("s_t23")
        s_nm = sem("s_nm")
        s_os = sem("s_os")
        s_at = sem("s_at")
        s_r = sem("s_r")
        s_mx = sem("s_mx")
        s_qk01 = sem("s_qk01")
        s_qk23 = sem("s_qk23")
        s_v = sem("s_v")
        s_rs = sem("s_rs")
        s_nrm = sem("s_nrm")
        s_up = sem("s_up")
        s_h = sem("s_h")
        s_dwn = sem("s_dwn")
        s_cmb = sem("s_cmb")
        s_res = sem("s_res")
        s_qb01 = sem("s_qb01")
        s_qb23 = sem("s_qb23")
        s_nmA = sem("s_nmA")
        s_nmB = sem("s_nmB")
        s_out = sem("s_out")

        def wait(eng, s, n):
            if not (isinstance(n, int) and n <= 0):
                eng.wait_ge(s, n)

        def batches(body, eng):
            for b in (-2, -1, 0, 1, 2):
                body(b, b % 2, F=b >= 1, A=b >= 0, N=b >= -1, Q=True)
            with eng.Fori(1, 6) as i:
                body(i * 2 + 1, 1, F=True, A=True, N=True, Q=True)
                body(i * 2 + 2, 0, F=True, A=True, N=True, Q=True)
            for b in (13, 14, 15, 16):
                body(b, b % 2, F=True, A=b <= 15, N=b <= 14, Q=b <= 13)

        block = ctx.enter_context(nc.Block())

        @block.sync
        def _(sp):
            xv = x.rearrange("b (t p) d -> p (b t) d", p=P)
            ov = out.rearrange("b (t p) d -> p (b t) d", p=P)
            for c in range(4):
                sp.dma_start(X[:, 8 * c:8 * c + 8, :], xv[:, 8 * c:8 * c + 8, :]).then_inc(s_x[c], 16)
            for dst, src in ((wst[:], wqkvT), (rows[0:1, 0:384], bqkv), (rows[0:1, 384:512], bproj),
                             (Wp[:], wprojT), (Wr[:], w_router)):
                sp.dma_start(dst, src).then_inc(s_w, 16)
            for e in range(FFNS):
                if e >= 2:
                    sp.wait_ge(s_ul, e - 1)
                sp.dma_start(ust[:, e % 2, :], w_sup if e == 0 else w_up[e - 1]).then_inc(s_u[e % 2], 16)
            sp.dma_start(Dn[:, 0], w_sdown.rearrange("(c p) d -> p c d", p=P)).then_inc(s_dn, 16)
            for e in range(E):
                sp.dma_start(Dn[:, e + 1], w_down[e].rearrange("(c p) d -> p c d", p=P)).then_inc(s_dn, 16)

            def spread(n, r, done):
                for q in range(LANES):
                    sp.dma_start(Qb[32 * q:32 * q + 32, r, 2 * n:2 * n + 2, q, :].bitcast(F32),
                                 Qd[32 * q:32 * q + 32, 2 * n:2 * n + 2, :].bitcast(F32)).then_inc(done, 16)

            def maxima(n, r, done):
                for q in range(LANES):
                    sp.dma_start(Qb[32 * q:32 * q + 1, r, 2 * n:2 * n + 2, q, :].bitcast(F32),
                                 NM[2 * q:2 * q + 2, n, :].bitcast(F32)).then_inc(done, 16)

            def body(b, r, F, A, N, Q):
                if N:
                    sp.wait_ge(s_qk23, 2 * (b + 1) + 1)
                    spread(1, 1 - r, s_qb23)
                if A:
                    sp.wait_ge(s_nm, 2 * b + 2)
                    maxima(1, r, s_nmB)
                if F:
                    sp.wait_ge(s_res, b)
                    lo = (b - 1) * TT
                    sp.dma_start(ov[:, bass.ds(lo, TT), :], X[:, bass.ds(lo, TT), :]).then_inc(s_out, 16)
                if Q:
                    sp.wait_ge(s_qk01, 2 * (b + 2) + 1)
                    spread(0, r, s_qb01)
                if N:
                    sp.wait_ge(s_nm, 2 * (b + 1) + 1)
                    maxima(0, 1 - r, s_nmA)

            batches(body, sp)
            sp.wait_ge(s_out, 16 * B)

        @block.gpsimd
        def _(pool):
            nc.gpsimd.memset(ident[:], 0.0).then_inc(s_id, 1)
            nc.gpsimd.memset(V[:], 0.0).then_inc(s_id, 1)
            pool.wait_ge(s_id, 2)
            nc.gpsimd.affine_select(out=ident[:], in_=ident[:], compare_op=ALU.not_equal, fill=1.0, base=0,
                                    pattern=[[-1, P]], channel_multiplier=1).then_inc(s_id, 1)
            nc.gpsimd.memset(V[:, :, :, :, 8:9], 1.0).then_inc(s_id, 1)
            nc.gpsimd.memset(Qb[:].bitcast(F32), 0.0).then_inc(s_set, 1)
            with pool.Fori(0, 4) as i:
                for r in range(2):
                    pool.wait_ge(s_xf, i * 2 + r + 1)
                    nc.gpsimd.tensor_copy(xTh[:, bass.ds(i * 1024 + r * 512, 512)], xf[:, r, :]).then_inc(s_hi, 1)
            pool.wait_ge(s_bias, 2)
            pool.wait_ge(s_xn, 8)
            nc.gpsimd.tensor_tensor(X[:], X[:], BVP[:, D:].unsqueeze(1).to_broadcast([P, TILES, D]), ALU.add).then_inc(s_xb, 1)
            pool.wait_ge(s_lo, 8)
            pool.wait_ge(s_hi, 8)
            pool.wait_ge(s_comb, 1)

            def fetch(b, r):
                nc.gpsimd.tensor_copy(xch[:, r, :], xTh[:, bass.ds(b * T, T)].bitcast(F32)).then_inc(s_xc, 1)
                nc.gpsimd.tensor_copy(xcl[:, r, :], xTl[:, bass.ds(b * T, T)].bitcast(F32)).then_inc(s_xc, 1)
                nc.gpsimd.tensor_copy(ccur[:, r, :],
                                      comb[:].rearrange("p t e -> p (t e)")[:, bass.ds(b * TT * E, TT * E)]).then_inc(s_xc, 1)

            fetch(0, 0)
            fetch(1, 1)
            with pool.Fori(1, 8) as i:
                for r in range(2):
                    pool.wait_ge(s_up, (i * 2 + r - 1) * NC)
                    pool.wait_ge(s_cmb, (i * 2 + r - 1) * NE)
                    fetch(i * 2 + r, r)

        @block.scalar
        def _(act):
            for e in range(FFNS):
                act.wait_ge(s_u[e % 2], 16 * (e // 2 + 1))
                nc.scalar.activation(Uh[:, e, :], ust[:, e % 2, :], ACT.Copy).then_inc(s_uh, 1)
            act.wait_ge(s_stat, 1)
            nc.scalar.activation(nrm[:, 1, :], nrm[:, 0, :], ACT.Sqrt).then_inc(s_sq, 1)
            with act.Fori(0, 4) as i:
                for r in range(2):
                    act.wait_ge(s_xnT, i * 2 + r + 1)
                    nc.scalar.activation(xf[:, r, :], sbank[r][:], ACT.Copy).then_inc(s_xf, 1)
                    act.wait_ge(s_lg, i * 2 + r + 1)
                    nc.scalar.activation(pr[:].rearrange("p t e -> p (t e)")[:, bass.ds(i * 64 + r * 32, 32)],
                                         tbank[r][:, 0:32], ACT.Exp, scale=-1.0).then_inc(s_pe_, 1)

            def ffn(b, r, k):
                for kind, e, c in FILL[k]:
                    if kind == "up":
                        n = CHUNK_OF[e, c]
                        act.wait_ge(s_up, b * NC + n + 1)
                        wait(act, s_h, b * NC + n - 1)
                        nc.scalar.activation(R[:, n % 2, :], ubank[:, 0:T], ACT.Relu).then_inc(s_r, 1)

            def partial(b, r, n, qk, produced, s_t, freed):
                act.wait_ge(produced, 2 * b + qk + 1)
                wait(act, freed[0], freed[1])
                for g in range(2):
                    ins = nc.scalar.activation(tmp[:, qk, g, :], misc[:, g * T:g * T + T], ACT.Identity,
                                               bias=bias[:, 10 + 4 * qk + 2 * n + g:11 + 4 * qk + 2 * n + g],
                                               scale=bias[:, 8 + qk:9 + qk])
                ins.then_inc(s_t, 1)

            def body(b, r, F, A, N, Q):
                for j in range(SLOTS):
                    if A:
                        for u in (2 * j, 2 * j + 1):
                            act.wait_ge(s_st, b * NU + u + 1)
                            wait(act, s_pv, b * 8 + j - 1)
                            nc.scalar.activation(PT[:, u % 4, :], tbank[u % 2][:], ACT.Exp, scale=SCALE).then_inc(s_e, 1)
                    if N and j < 2:
                        partial(b + 1, 1 - r, 1, j, s_p23, s_t23, (s_qk01, 2 * (b + 1) + j + 1))
                    if Q and j in (4, 5):
                        partial(b + 2, r, 0, j - 4, s_p01, s_t01, (s_qk23, 2 * (b + 1) + j - 3))
                    if F and j == 0:
                        act.wait_ge(s_pv, b * 8)
                        wait(act, s_tr, 2 * b - 2)
                        nc.scalar.activation(OS[:, 1], obank[:].rearrange("p (g q) -> p g q", g=2), ACT.Copy).then_inc(s_os, 1)
                    if A and j == 4:
                        act.wait_ge(s_pv, b * 8 + 4)
                        nc.scalar.activation(OS[:, 0], obank[:].rearrange("p (g q) -> p g q", g=2), ACT.Copy).then_inc(s_os, 1)
                    if N:
                        ffn(b + 1, 1 - r, 2 * j)
                    if A and j == 1:
                        act.wait_ge(s_mt, 2 * b + 2)
                        wait(act, s_nmB, 64 * b)
                        nc.scalar.activation(NM[:, 1, :], misc[0:8, 0:T], ACT.Copy).then_inc(s_nm, 1)
                    if N and j == 5:
                        act.wait_ge(s_mt, 2 * (b + 1) + 1)
                        wait(act, s_nmA, 64 * (b + 1))
                        nc.scalar.activation(NM[:, 0, :], misc[0:8, 0:T], ACT.Copy).then_inc(s_nm, 1)
                    if F and j == 2:
                        act.wait_ge(s_ant, b)
                        wait(act, s_y, b - 1)
                        nc.scalar.activation(AT[:], misc[:, 0:T], ACT.Copy).then_inc(s_at, 1)
                    if N:
                        ffn(b + 1, 1 - r, 2 * j + 1)

            batches(body, act)

        @block.vector
        def _(dve):
            chain = [0]

            def link(ins):
                chain[0] += 1
                ins.then_inc(s_dve, 1)
                dve.wait_ge(s_dve, chain[0])

            dve.wait_ge(s_w, 80)
            link(nc.vector.tensor_copy(wsh[:], wst[:]))
            nc.vector.memset(Wqh[:].bitcast(F32), 0.0)
            nc.vector.memset(Wql[:].bitcast(F32), 0.0)
            nc.vector.memset(rows[0:1, 512:2048], 0.0)
            nc.vector.memset(bias[:], 0.0)
            link(nc.vector.tensor_tensor(wsl[:], wst[:], wsh[:].bitcast(F32), ALU.subtract))
            for qk in range(2):
                for src, dst in ((wsh, Wqh), (wsl, Wql)):
                    for p in PART:
                        o = dst[:, qk].rearrange("p g (q c) -> p (g q) c", c=32)[:, :, p:p + 8]
                        i = src[:, qk * D:(qk + 1) * D].bitcast(F32).rearrange("p (h d) -> p h d", d=HD)
                        nc.vector.tensor_copy(o, i)
                for p in PART:
                    o = rows[0:1, 512 + 512 * qk:1024 + 512 * qk].rearrange("p (h c) -> p h c", c=32)[:, :, p:p + 8]
                    nc.vector.tensor_copy(o, rows[0:1, qk * D:(qk + 1) * D].rearrange("p (h d) -> p h d", d=HD))
                p = PART[(QLO, KLO)[qk]]
                m = rows[0:1, 1536 + P * qk:1536 + P * qk + P].rearrange("p (q c) -> p q c", c=32)
                nc.vector.memset(m[:, :, p:p + 8], 1.0)
            nc.vector.memset(rows[0:1, 1024:1536].rearrange("p (h c) -> p h c", c=32)[:, :, 0:1], 1.0)
            nc.vector.memset(rows[0:1, 1792:1920], 1.0).then_inc(s_rows, 1)
            for c in range(4):
                dve.wait_ge(s_x[c], 16)
                for t in range(8 * c, 8 * c + 8):
                    nc.vector.bn_stats(st6[:, t, :], X[:, t, :]).then_inc(s_dve, 1)
            chain[0] += TILES
            dve.wait_ge(s_dve, chain[0])
            for t in range(TILES):
                nc.vector.bn_aggr(mv[:, t, :], st6[:, t, :]).then_inc(s_dve, 1)
            chain[0] += TILES
            dve.wait_ge(s_dve, chain[0])
            nc.vector.tensor_scalar(nrm[:, 0, :], mv[:, :, 1], EPS, None, ALU.add).then_inc(s_stat, 1)
            for e in range(FFNS):
                dve.wait_ge(s_uh, e + 1)
                nc.vector.tensor_tensor(Ul[:, e, :], ust[:, e % 2, :], Uh[:, e, :].bitcast(F32), ALU.subtract).then_inc(s_ul, 1)
            dve.wait_ge(s_sq, 1)
            link(nc.vector.reciprocal(nrm[:, 2, :], nrm[:, 1, :]))
            link(nc.vector.tensor_tensor(nrm[:, 3, :], nrm[:, 2, :], nrm[:, 2, :], ALU.mult))
            link(nc.vector.tensor_tensor(nrm[:, 3, :], nrm[:, 3, :], nrm[:, 0, :], ALU.mult))
            link(nc.vector.tensor_scalar(nrm[:, 3, :], nrm[:, 3, :], -0.5, 1.5, ALU.mult, ALU.add))
            link(nc.vector.tensor_tensor(nrm[:, 1, :], nrm[:, 3, :], nrm[:, 2, :], ALU.mult))
            dve.wait_ge(s_bps, 1)
            link(nc.vector.tensor_copy(bias[:, 0:10], misc[:, 0:10]))
            for qk in range(2):
                nc.vector.tensor_scalar(bias[:, 10 + 4 * qk:14 + 4 * qk], bias[:, 4 * qk:4 * qk + 4],
                                        bias[:, 8 + qk:9 + qk], None, ALU.mult)
            nc.vector.tensor_copy(BVP[:], misc[:, 128:384]).then_inc(s_bias, 2)
            Xf = X[:].rearrange("p t d -> p (t d)")
            mvf = mv[:].rearrange("p t c -> p (t c)")
            with dve.Fori(0, 4) as i:
                for r in range(2):
                    dve.wait_ge(s_xnT, i * 2 + r) if r else None
                    for t in range(CHUNK):
                        tile = i * 8 + (r * CHUNK + t)
                        ins = nc.vector.tensor_scalar(xn[:, r, t, :], Xf[:, bass.ds(tile * D, D)],
                                                      mvf[:, bass.ds(tile * 2, 1)], nrm[:, 1, bass.ds(tile, 1)],
                                                      ALU.subtract, ALU.mult)
                    ins.then_inc(s_xn, 1)
                for r in range(2):
                    dve.wait_ge(s_hi, i * 2 + r + 1)
                    cols = bass.ds(i * 1024 + r * 512, 512)
                    nc.vector.tensor_tensor(xTl[:, cols], xf[:, r, :], xTh[:, cols].bitcast(F32),
                                            ALU.subtract).then_inc(s_lo, 1)
            for e in range(E):
                nc.vector.memset(wte[:, e:e + 1], float(E - e))
            dve.wait_ge(s_pe_, 8)
            def bc(ap):
                return ap.unsqueeze(2).to_broadcast([P, TILES, E])
            wt = wte[:].unsqueeze(1).to_broadcast([P, TILES, E])
            link(nc.vector.tensor_scalar(pr[:], pr[:], 1.0, None, ALU.add))
            link(nc.vector.reciprocal(pr[:], pr[:]))
            src = pr[:]
            for k in range(2):
                link(nc.vector.tensor_reduce(rm[:, k, :], src, AX_X, ALU.max))
                link(nc.vector.tensor_tensor(rt[:, 4], src, bc(rm[:, k, :]), ALU.is_equal))
                link(nc.vector.tensor_tensor(rt[:, 4], rt[:, 4], wt, ALU.mult))
                link(nc.vector.tensor_reduce(rm[:, 2, :], rt[:, 4], AX_X, ALU.max))
                link(nc.vector.tensor_tensor(rt[:, k], rt[:, 4], bc(rm[:, 2, :]), ALU.is_equal))
                if k == 0:
                    link(nc.vector.tensor_scalar(rt[:, 2], rt[:, 0], -2.0, None, ALU.mult))
                    link(nc.vector.tensor_tensor(rt[:, 2], rt[:, 2], pr[:], ALU.add))
                    src = rt[:, 2]
            link(nc.vector.tensor_tensor(rm[:, 2, :], rm[:, 0, :], rm[:, 1, :], ALU.add))
            link(nc.vector.tensor_scalar(rm[:, 2, :], rm[:, 2, :], 1e-6, None, ALU.add))
            link(nc.vector.reciprocal(rm[:, 3, :], rm[:, 2, :]))
            for k in range(2):
                link(nc.vector.tensor_tensor(rm[:, k, :], rm[:, k, :], rm[:, 3, :], ALU.mult))
                link(nc.vector.tensor_tensor(rt[:, k], rt[:, k], bc(rm[:, k, :]), ALU.mult))
            nc.vector.tensor_tensor(comb[:], rt[:, 0], rt[:, 1], ALU.add).then_inc(s_comb, 1)
            dve.wait_ge(s_xb, 1)

            def ffn(b, r, k):
                for kind, e, c in FILL[k]:
                    if kind == "up":
                        n = CHUNK_OF[e, c]
                        dve.wait_ge(s_r, b * NC + n + 1)
                        wait(dve, s_dwn, b * NE + e - 1)
                        nc.vector.tensor_tensor(hT[:, (r + e) % 2, c, :], R[:, n % 2, :], R[:, n % 2, :],
                                                ALU.mult).then_inc(s_h, 1)
                    else:
                        y = ybank[:, 0:T]
                        dve.wait_ge(s_dwn, b * NE + e + 1)
                        wait(dve, s_cmb, b * NE + e)
                        for t in range(TT):
                            o = Xf[:, bass.ds((b * TT + t) * D, D)]
                            if e == 0:
                                ins = nc.vector.tensor_tensor(o, y[:, t * D:t * D + D], o, ALU.add)
                            else:
                                ins = nc.vector.scalar_tensor_tensor(
                                    out=o, in0=y[:, t * D:t * D + D], scalar=ccur[:, r, t * E + e - 1:t * E + e],
                                    in1=o, op0=ALU.mult, op1=ALU.add)
                        ins.then_inc(s_cmb, 1)

            def split(b, r, n, qk, s_t, done):
                dve.wait_ge(s_t, 2 * b + qk + 1)
                if qk == 0:
                    wait(dve, (s_qb01, s_qb23)[n], 64 * b)
                for g in range(2):
                    dst = Qd[:, 2 * n + g, :] if qk == 0 else Kd[:, r, 2 * n + g, :]
                    ins = nc.vector.scalar_tensor_tensor(
                        out=dst, in0=misc[:, g * T:g * T + T], scalar=bias[:, 4 * qk + 2 * n + g:4 * qk + 2 * n + g + 1],
                        in1=tmp[:, qk, g, :].bitcast(F32), op0=ALU.add, op1=ALU.subtract)
                ins.then_inc(done, 1)

            def normalise(b, n):
                dve.wait_ge(s_tr, 2 * b + n + 1)
                wait(dve, s_ant, b)
                m = misc[:].rearrange("p (q h c) -> p q h c", q=TT, c=32)
                nc.vector.reciprocal(rs[:, n, :].rearrange("p (q h c) -> p q h c", q=TT, c=1), m[:, :, :, 8:9]).then_inc(s_rs, 1)
                dve.wait_ge(s_rs, 2 * b + n + 1)
                nc.vector.tensor_tensor(
                    AN[:, :, 64 * n:64 * n + 64].rearrange("p q (h d) -> p q h d", d=HD), m[:, :, :, 0:8],
                    rs[:, n, :].rearrange("p (q h) -> p q h", q=TT).unsqueeze(3).to_broadcast([P, TT, 8, HD]),
                    ALU.mult).then_inc(s_nrm, 1)

            def body(b, r, F, A, N, Q):
                for j in range(SLOTS):
                    if N and j < 2:
                        split(b + 1, 1 - r, 1, j, s_t23, s_qk23)
                    if N and j == 2:
                        dve.wait_ge(s_vps, b + 2)
                        nc.vector.tensor_tensor(
                            V[:, 1 - r, :, :, 0:8], misc[:, 0:2 * D].rearrange("p (t h d) -> p t h d", t=TT, d=HD),
                            BVP[:, 0:D].rearrange("p (h d) -> p h d", d=HD).unsqueeze(1).to_broadcast([P, TT, NH, HD]),
                            ALU.add).then_inc(s_v, 1)
                    if Q and j in (4, 5):
                        split(b + 2, r, 0, j - 4, s_t01, s_qk01)
                    for half in range(2):
                        if N:
                            h = 2 * j + half
                            dve.wait_ge(s_s, (b + 1) * NU + h + 1)
                            wait(dve, s_mt, 2 * (b + 1) - 1 + h // 8)
                            nc.vector.tensor_reduce(Mx[:, h // 8, :, h % 4, (h // 4) % 2],
                                                    sbank[h % 2][:].rearrange("p (q k) -> p q k", q=TT), AX_X, ALU.max,
                                                    negate=True).then_inc(s_mx, 1)
                        if half == 1:
                            if F and j == 0:
                                normalise(b - 1, 1)
                            if A and j == 4:
                                normalise(b, 0)
                            if F and j == 3:
                                dve.wait_ge(s_y, b)
                                wait(dve, s_cmb, b * NE)
                                o = Xf[:, bass.ds((b - 1) * TT * D, TT * D)]
                                nc.vector.tensor_tensor(o, misc[:, 0:T], o, ALU.add).then_inc(s_res, 1)
                        if N:
                            ffn(b + 1, 1 - r, 2 * j + half)

            batches(body, dve)

        @block.tensor
        def _(pe):
            pe.wait_ge(s_id, 3)
            pe.wait_ge(s_rows, 1)
            one = rows[0:1, 1792:1793]
            for qk in range(2):
                for g in range(GROUPS):
                    a = 512 + 512 * qk + P * g
                    nc.tensor.matmul(misc[:, 4 * qk + g:4 * qk + g + 1], rows[0:1, a:a + P], one, start=True, stop=True)
                a = 1536 + P * qk
                nc.tensor.matmul(misc[:, 8 + qk:9 + qk], rows[0:1, a:a + P], one, start=True, stop=True)
            nc.tensor.matmul(misc[:, 128:384], rows[0:1, 1792:1920], rows[0:1, 256:512],
                             start=True, stop=True).then_inc(s_bps, 1)
            with pe.Fori(0, 4) as i:
                for r in range(2):
                    pe.wait_ge(s_xn, i * 2 + r + 1)
                    for t in range(CHUNK):
                        ins = nc.tensor.transpose(sbank[r][:, t * P:t * P + P], xn[:, r, t, :], ident[:])
                    ins.then_inc(s_xnT, 1)
                for r in range(2):
                    pe.wait_ge(s_xf, i * 2 + r + 1)
                    for t in range(CHUNK):
                        ins = nc.tensor.matmul(tbank[r][:, t * E:t * E + E], xf[:, r, t * P:t * P + P], Wr[:],
                                               start=True, stop=True)
                    ins.then_inc(s_lg, 1)
            pe.wait_ge(s_ul, FFNS)
            pe.wait_ge(s_dn, 16 * FFNS)
            pe.wait_ge(s_bias, 2)
            pe.wait_ge(s_id, 4)
            pe.wait_ge(s_set, 1)
            pe.wait_ge(s_pe_, 8)

            def three(o, lh, ll, rh, rl):
                nc.tensor.matmul(o, lh, rl, start=True, stop=False)
                nc.tensor.matmul(o, ll, rh, start=False, stop=False)
                return nc.tensor.matmul(o, lh, rh, start=False, stop=True)

            def ffn(b, r, k):
                for kind, e, c in FILL[k]:
                    if kind == "up":
                        n = CHUNK_OF[e, c]
                        wait(pe, s_r, b * NC + n)
                        ins = three(ubank[:, 0:T], Uh[:, e, c * P:c * P + P],
                                    Ul[:, e, c * P:c * P + P], xch[:, r, :], xcl[:, r, :])
                        ins.then_inc(s_up, 1)
                    else:
                        y = ybank[:, 0:T]
                        pe.wait_ge(s_h, b * NC + (e + 1) * HC)
                        wait(pe, s_cmb, b * NE + e)
                        for t in range(TT):
                            for c in range(HC):
                                ins = nc.tensor.matmul(y[:, t * D:t * D + D], hT[:, (r + e) % 2, c, t * P:t * P + P],
                                                       Dn[:, e, c, :], start=c == 0, stop=c == HC - 1)
                        ins.then_inc(s_dwn, 1)

            def project(b, r, n, qk, done):
                wait(pe, s_xc, 3 * (b + 1))
                for g in range(2):
                    w = 2 * n + g
                    ins = three(misc[:, g * T:g * T + T], Wqh[:, qk, w, :], Wql[:, qk, w, :], xch[:, r, :], xcl[:, r, :])
                ins.then_inc(done, 1)

            def turn(b, n):
                pe.wait_ge(s_os, 2 * b + n + 1)
                for t in range(TT):
                    for g in range(2):
                        ins = nc.tensor.transpose(misc[:, (2 * t + g) * P:(2 * t + g) * P + P],
                                                  OS[:, n, g, t * P:t * P + P], ident[:])
                ins.then_inc(s_tr, 1)

            def turn_max(b, n):
                pe.wait_ge(s_mx, b * NU + 8 * n + 8)
                for t in range(TT):
                    ins = nc.tensor.transpose(misc[0:8, t * P:t * P + P],
                                              Mx[:, n, t].rearrange("p q g -> p (q g)"), ident[:])
                ins.then_inc(s_mt, 1)

            def body(b, r, F, A, N, Q):
                for j in range(SLOTS):
                    if A:
                        if j == 0:
                            pe.wait_ge(s_nmA, 64 * (b + 1))
                        if j == 4:
                            pe.wait_ge(s_nmB, 64 * (b + 1))
                        for u in (2 * j, 2 * j + 1):
                            g, kt, half = u // 4, (u // 2) % 2, u % 2
                            wait(pe, s_e, b * NU + u - 1)
                            nc.tensor.matmul(tbank[u % 2][:], Kd[:, r, g, kt * P:kt * P + P],
                                             Qb[:, r, g, 2 * half:2 * half + 2, :], start=True, stop=True).then_inc(s_st, 1)
                    if N and j == 0:
                        wait(pe, s_qk01, 2 * (b + 1) + 2)
                        if A:
                            pe.wait_ge(s_nm, 2 * b + 1)
                        project(b + 1, 1 - r, 1, 0, s_p23)
                    if N and j == 1:
                        pe.wait_ge(s_qk23, 2 * (b + 1) + 1)
                        if F:
                            pe.wait_ge(s_nrm, 2 * b)
                        project(b + 1, 1 - r, 1, 1, s_p23)
                    if N and j == 2:
                        pe.wait_ge(s_qk23, 2 * (b + 1) + 2)
                        if A:
                            pe.wait_ge(s_nm, 2 * b + 2)
                        for t in range(TT):
                            ins = three(misc[:, t * D:t * D + D], xch[:, 1 - r, t * P:t * P + P],
                                        xcl[:, 1 - r, t * P:t * P + P], wsh[:, 2 * D:], wsl[:, 2 * D:])
                        ins.then_inc(s_vps, 1)
                    if Q and j == 4:
                        if N:
                            pe.wait_ge(s_v, b + 2)
                        if F:
                            pe.wait_ge(s_res, b)
                        project(b + 2, r, 0, 0, s_p01)
                    if Q and j == 5:
                        pe.wait_ge(s_qk01, 2 * (b + 2) + 1)
                        if A:
                            pe.wait_ge(s_nrm, 2 * b + 1)
                        project(b + 2, r, 0, 1, s_p01)
                    for half in range(2):
                        if N:
                            h = 2 * j + half
                            g, q = h // 4, h % 4
                            if h == 0:
                                pe.wait_ge(s_qk01, 2 * (b + 1) + 2)
                                pe.wait_ge(s_qb01, 64 * (b + 2))
                            if h == 8:
                                pe.wait_ge(s_qk23, 2 * (b + 1) + 2)
                                pe.wait_ge(s_qb23, 64 * (b + 2))
                            wait(pe, s_mx, (b + 1) * NU + h - 1)
                            for t in range(TT):
                                ins = nc.tensor.matmul(sbank[h % 2][:, t * T:t * T + T],
                                                       Qb[:, 1 - r, g, q, t * P:t * P + P], Kd[:, 1 - r, g, :],
                                                       start=True, stop=True)
                            ins.then_inc(s_s, 1)
                        if half == 1:
                            if F and j == 0:
                                if N:
                                    pe.wait_ge(s_qk23, 2 * (b + 1) + 1)
                                elif A:
                                    pe.wait_ge(s_nm, 2 * b + 1)
                                else:
                                    pe.wait_ge(s_nrm, 2 * b - 1)
                                turn(b - 1, 1)
                            if A and j == 1:
                                if N:
                                    pe.wait_ge(s_qk23, 2 * (b + 1) + 2)
                                if F:
                                    pe.wait_ge(s_nrm, 2 * b)
                                turn_max(b, 1)
                            if F and j == 2:
                                if N:
                                    pe.wait_ge(s_v, b + 2)
                                if A:
                                    pe.wait_ge(s_nm, 2 * b + 2)
                                pe.wait_ge(s_nrm, 2 * b)
                                for t in range(TT):
                                    ins = nc.tensor.transpose(misc[:, t * P:t * P + P], AN[:, t, :], ident[:])
                                ins.then_inc(s_ant, 1)
                            if F and j == 3:
                                pe.wait_ge(s_at, b)
                                for t in range(TT):
                                    ins = nc.tensor.matmul(misc[:, t * D:t * D + D], AT[:, t * P:t * P + P], Wp[:],
                                                           start=True, stop=True)
                                ins.then_inc(s_y, 1)
                            if A and j == 4:
                                if Q:
                                    pe.wait_ge(s_qk01, 2 * (b + 2) + 1)
                                if F:
                                    pe.wait_ge(s_res, b)
                                if N:
                                    pe.wait_ge(s_v, b + 2)
                                turn(b, 0)
                            if N and j == 5:
                                if Q:
                                    pe.wait_ge(s_qk01, 2 * (b + 2) + 2)
                                if A:
                                    pe.wait_ge(s_nrm, 2 * b + 1)
                                turn_max(b + 1, 0)
                        if N:
                            ffn(b + 1, 1 - r, 2 * j + half)
                    if A:
                        g, kt = j // 2, j % 2
                        pe.wait_ge(s_e, b * NU + 2 * j + 2)
                        if j == 0:
                            pe.wait_ge(s_v, b + 1)
                            wait(pe, s_os, 2 * b)
                        if j == 4:
                            pe.wait_ge(s_os, 2 * b + 1)
                        for q in range(LANES):
                            ins = nc.tensor.matmul(obank[32 * q:32 * q + 32, (g % 2) * T:(g % 2) * T + T],
                                                   V[:, r, kt, 4 * g + q, :],
                                                   PT[:, (2 * j + q // 2) % 4, (q % 2) * T:(q % 2) * T + T],
                                                   start=kt == 0, stop=kt == 1)
                        ins.then_inc(s_pv, 1)

            batches(body, pe)


def kernel(L0_attn_x, L0_attn_qkv_w, L0_attn_qkv_b, L0_attn_proj_w, L0_attn_proj_b, L0_ffn_W_router,
           L0_ffn_W_up, L0_ffn_W_down, L0_ffn_W_sh_up, L0_ffn_W_sh_down):
    import numpy as np
    import concourse.bacc as bacc
    from concourse.bass_utils import run_bass_kernel_spmd

    nc = bacc.Bacc("TRN2", target_bir_lowering=False, num_devices=1)
    given = {
        "x": L0_attn_x, "wqkvT": np.transpose(L0_attn_qkv_w), "bqkv": np.reshape(L0_attn_qkv_b, (1, -1)),
        "wprojT": np.transpose(L0_attn_proj_w), "bproj": np.reshape(L0_attn_proj_b, (1, -1)),
        "w_router": L0_ffn_W_router, "w_up": L0_ffn_W_up, "w_down": L0_ffn_W_down,
        "w_sup": L0_ffn_W_sh_up, "w_sdown": L0_ffn_W_sh_down,
    }
    arrays = {f"in_{k}": np.ascontiguousarray(v) for k, v in given.items()}
    args = [nc.dram_tensor(n, a.shape, F32, kind="ExternalInput").ap() for n, a in arrays.items()]
    out = nc.dram_tensor("out_0", (B, T, D), F32, kind="ExternalOutput").ap()
    build(nc, *args, out)
    return run_bass_kernel_spmd(nc, [arrays], core_ids=[0]).results[0]["out_0"]
```

```python
from contextlib import ExitStack

import concourse.bass as bass
from concourse import mybir

F32 = mybir.dt.float32
F32R = mybir.dt.float32r
I32 = mybir.dt.int32
ALU = mybir.AluOpType
ACT = mybir.ActivationFunctionType
AX_X = mybir.AxisListType.X

P = 128
B, T, D = 16, 256, 128
NH, HD = 16, 8
GROUPS, LANES = 4, 4
TT = T // P
TILES = B * TT
E, H = 8, 512
HC = H // P
FFNS = E + 1
SCALE = HD ** -0.5
EPS = 1e-5
SLOTS = 8
VW = HD + 1
CHUNK = 4
PART = [8, 16, 24]
QLO, KLO = 1, 2

NU = 16
NC = 2
NT = TILES * 2 + E
LATE = FFNS - 4
ROUTED_AT = 6
FILL = {4: ("up", 0), 8: ("up", 1), 15: ("down", 0)}
FINAL = {13: ((6, 2), (7, 4), (8, 6)), 14: ((9, 1), (10, 4), (11, 7)), 15: ((12, 3), (13, 6)), 16: ((14, 3),)}


def build(nc, x, wqkvT, bqkv, wprojT, bproj, w_router, w_up, w_down, w_sup, w_sdown, slots, results, out):
    with ExitStack() as ctx:
        def sb(name, shape, dt=F32):
            return ctx.enter_context(nc.sbuf_tensor(name, shape, dt))

        def bank(name):
            return ctx.enter_context(nc.psum_tensor(name, [P, 512], F32))

        def sem(name):
            return ctx.enter_context(nc.semaphore(name))

        X = sb("X", [P, TILES, D])
        xTh = sb("xTh", [P, B * T], F32R)
        xTl = sb("xTl", [P, B * T], F32R)
        Uh = sb("Uh", [P, FFNS, H], F32R)
        Ul = sb("Ul", [P, FFNS, H], F32R)
        Dn = sb("Dn", [P, FFNS, HC, D])
        Wqh = sb("Wqh", [P, 2, GROUPS, P], F32R)
        Wql = sb("Wql", [P, 2, GROUPS, P], F32R)
        wsh = sb("wsh", [P, 3 * D], F32R)
        wsl = sb("wsl", [P, 3 * D], F32R)
        Wp = sb("Wp", [P, D])
        Wr = sb("Wr", [P, E])
        ident = sb("ident", [P, P])
        bias = sb("bias", [P, 20])
        BVP = sb("BVP", [P, 2 * D])
        st6 = sb("st6", [P, TILES, 6])
        mv = sb("mv", [P, TILES, 2])
        nrm = sb("nrm", [P, 4, TILES])
        rm = sb("rm", [P, 4, TILES])
        wte = sb("wte", [P, E])
        cnt = sb("cnt", [P, 6, E])
        thr = sb("thr", [P, TILES])
        tix = sb("tix", [1, NT])
        tex = sb("tex", [1, NT])
        texi = sb("texi", [1, NT], I32)
        pos = sb("pos", [P, 2, TILES], I32)
        Wrh = sb("Wrh", [P, E], F32R)
        Wrl = sb("Wrl", [P, E], F32R)
        xrh = sb("xrh", [P, 2, P], F32R)
        xrl = sb("xrl", [P, 2, P], F32R)
        ys = sb("ys", [P, 2, D])
        G = sb("G", [P, 2, 2 * TT, D])
        xch = sb("xch", [P, 2, T], F32R)
        xcl = sb("xcl", [P, 2, T], F32R)
        xr = sb("xr", [P, 2, TT * D])
        Qd = sb("Qd", [P, GROUPS, T], F32R)
        tmp = sb("tmp", [P, 2, 2, T], F32R)
        Kd = sb("Kd", [P, 2, GROUPS, T], F32R)
        Qb = sb("Qb", [P, 2, GROUPS, LANES, T], F32R)
        V = sb("V", [P, 2, TT, NH * VW + 32 - VW + 1])
        PT = sb("PT", [P, 4, 512])
        Mx = sb("Mx", [P, 2, TT, LANES, 2])
        NM = sb("NM", [8, 2, T], F32R)
        OS = sb("OS", [P, 2, 2, T])
        rs = sb("rs", [P, 2, 2 * TT * LANES])
        AN = sb("AN", [P, TT, D])
        AT = sb("AT", [P, T])
        R = sb("R", [P, 2 * T])
        hT = sb("hT", [P, HC, T])

        rows = PT[0:1].rearrange("p a b -> p (a b)")
        ust = OS[:].rearrange("p a b c -> p a (b c)")
        sel = G[:, 0, 0:2, :]
        wst = G[:, 1].rearrange("p a d -> p (a d)")[:, 0:3 * D]
        rr = PT[:, 0:2, :]
        hr = PT[:, 2:4, :].rearrange("p r (c m) -> p r c m", c=HC)
        xs = R[:].rearrange("p (k d) -> p k d", k=4)

        def table(k):
            w = TILES * E
            return Dn[:, LATE:].rearrange("p e c d -> p (e c d)")[:, k * w:k * w + w].rearrange("p (t e) -> p t e", e=E)

        sbank = [bank("sbank0"), bank("sbank1")]
        tbank = [bank("tbank0"), bank("tbank1")]
        obank = bank("obank")
        pbank = bank("pbank")
        wbank = bank("wbank")
        fbank = bank("fbank")

        s_x = [sem(f"s_x{c}") for c in range(4)]
        s_w = [sem(f"s_w{c}") for c in range(5)]
        s_u = [sem("s_u0"), sem("s_u1")]
        s_uh = sem("s_uh")
        s_ul = sem("s_ul")
        s_dn = sem("s_dn")
        s_dn0 = sem("s_dn0")
        s_id = sem("s_id")
        s_vz = sem("s_vz")
        s_qz = sem("s_qz")
        s_zero = sem("s_zero")
        s_wr = sem("s_wr")
        s_rows = sem("s_rows")
        s_bps = sem("s_bps")
        s_bias = sem("s_bias")
        s_stat = sem("s_stat")
        s_sq = sem("s_sq")
        s_xn = sem("s_xn")
        s_xnT = sem("s_xnT")
        s_hi = sem("s_hi")
        s_lo = sem("s_lo")
        s_lg = sem("s_lg")
        s_sig = sem("s_sig")
        s_dve = sem("s_dve")
        s_sel = sem("s_sel")
        s_M = sem("s_M")
        s_cnt = sem("s_cnt")
        s_cntr = sem("s_cntr")
        s_tex = sem("s_tex")
        s_pos = sem("s_pos")
        s_scat = [sem("s_scat0"), sem("s_scat1")]
        s_xs = [sem(f"s_xs{c}") for c in range(4)]
        s_xt = sem("s_xt")
        s_xh = sem("s_xh")
        s_xl = sem("s_xl")
        s_hu = sem("s_hu")
        s_rr = sem("s_rr")
        s_ht = sem("s_ht")
        s_hr = sem("s_hr")
        s_yd = sem("s_yd")
        s_ys = sem("s_ys")
        s_yst = [sem("s_yst0"), sem("s_yst1")]
        s_G = [sem("s_G0"), sem("s_G1")]
        s_fin = sem("s_fin")
        s_f0 = sem("s_f0")
        s_xc = sem("s_xc")
        s_xrl = [sem("s_xr0"), sem("s_xr1")]
        s_xrb = sem("s_xrb")
        s_st = sem("s_st")
        s_s = sem("s_s")
        s_pv = sem("s_pv")
        s_tr = sem("s_tr")
        s_ant = sem("s_ant")
        s_y = sem("s_y")
        s_mt = sem("s_mt")
        s_p01 = sem("s_p01")
        s_p23 = sem("s_p23")
        s_vps = sem("s_vps")
        s_e = sem("s_e")
        s_t01 = sem("s_t01")
        s_t23 = sem("s_t23")
        s_nm = sem("s_nm")
        s_os = sem("s_os")
        s_at = sem("s_at")
        s_r = sem("s_r")
        s_mx = sem("s_mx")
        s_qk01 = sem("s_qk01")
        s_qk23 = sem("s_qk23")
        s_v = sem("s_v")
        s_rs = sem("s_rs")
        s_nrm = sem("s_nrm")
        s_up = sem("s_up")
        s_h = sem("s_h")
        s_dwn = sem("s_dwn")
        s_cmb = sem("s_cmb")
        s_res = sem("s_res")
        s_qb01 = sem("s_qb01")
        s_qb23 = sem("s_qb23")
        s_nmA = sem("s_nmA")
        s_nmB = sem("s_nmB")
        s_out = sem("s_out")

        def wait(eng, s, n):
            if not (isinstance(n, int) and n <= 0):
                eng.wait_ge(s, n)

        def batches(body, eng, after=None, routed=None):
            for b in (-2, -1, 0, 1, 2):
                body(b, b % 2, F=b >= 1, A=b >= 0, N=b >= -1, Q=True, S=False)
                if after:
                    after(b)
            with eng.Fori(1, 3) as i:
                body(i * 2 + 1, 1, F=True, A=True, N=True, Q=True, S=False)
                body(i * 2 + 2, 0, F=True, A=True, N=True, Q=True, S=False)
            if routed:
                routed()
            with eng.Fori(3, 6) as i:
                body(i * 2 + 1, 1, F=True, A=True, N=True, Q=True, S=True)
                body(i * 2 + 2, 0, F=True, A=True, N=True, Q=True, S=True)
            for b in (13, 14, 15, 16):
                body(b, b % 2, F=True, A=b <= 15, N=b <= 14, Q=b <= 13, S=True)

        def steps(step, eng):
            for s in range(7):
                step(s, 0, s)
            with eng.Fori(0, (NT - 8) // 4) as i:
                for c in range(7, 11):
                    step(i * 4 + c, i, c)
            for s in range(NT - 1, NT + 3):
                step(s, 0, s)

        def within(s, lag):
            return not isinstance(s, int) or lag <= s < NT + lag

        def finals(b):
            return FINAL.get(b, ()) if isinstance(b, int) else ((b - (ROUTED_AT + 1), 4),)

        block = ctx.enter_context(nc.Block())

        @block.sync
        def _(sp):
            xv = x.rearrange("b (t p) d -> p (b t) d", p=P)
            ov = out.rearrange("b (t p) d -> p (b t) d", p=P)
            for c in range(4):
                sp.dma_start(X[:, 8 * c:8 * c + 8, :], xv[:, 8 * c:8 * c + 8, :]).then_inc(s_x[c], 16)
            for k, (dst, src) in enumerate(((wst[:], wqkvT), (rows[0:1, 0:384], bqkv), (rows[0:1, 384:512], bproj),
                                            (Wr[:], w_router), (Wp[:], wprojT))):
                sp.dma_start(dst, src).then_inc(s_w[k], 16)
            for e in range(FFNS):
                if e >= 2:
                    sp.wait_ge(s_ul, e - 1)
                sp.dma_start(ust[:, e % 2, :], w_sup if e == 0 else w_up[e - 1]).then_inc(s_u[e % 2], 16)
            sp.dma_start(Dn[:, 0], w_sdown.rearrange("(c p) d -> p c d", p=P)).then_inc(s_dn0, 16)
            sp.wait_ge(s_qz, 1)
            zero = Qb[:].bitcast(F32).rearrange("p a b c d -> p (a b c d)")[:, 0:NT * D // 2]
            half = NT * P // 2
            for k in range(2):
                sp.dma_start(slots[k * half:k * half + half].rearrange("(p t) d -> p (t d)", p=P),
                             zero).then_inc(s_zero, 16)
            sp.wait_ge(s_zero, 32)
            for e in range(LATE - 1):
                sp.dma_start(Dn[:, e + 1], w_down[e].rearrange("(c p) d -> p c d", p=P)).then_inc(s_dn, 16)

            def residual(b, r):
                sp.dma_start(xr[:, r, :].rearrange("p (t d) -> p t d", t=TT),
                             xv[:, bass.ds(b * TT, TT), :]).then_inc(s_xrl[r], 16)

            def spread(n, r, done):
                for q in range(LANES):
                    sp.dma_start(Qb[32 * q:32 * q + 32, r, 2 * n:2 * n + 2, q, :].bitcast(F32),
                                 Qd[32 * q:32 * q + 32, 2 * n:2 * n + 2, :].bitcast(F32)).then_inc(done, 16)

            def maxima(n, r, done):
                for q in range(LANES):
                    sp.dma_start(Qb[32 * q:32 * q + 1, r, 2 * n:2 * n + 2, q, :].bitcast(F32),
                                 NM[2 * q:2 * q + 2, n, :].bitcast(F32)).then_inc(done, 16)

            def body(b, r, F, A, N, Q, S):
                if A:
                    sp.wait_ge(s_nm, 2 * b + 2)
                    maxima(1, r, s_nmB)
                if N:
                    sp.wait_ge(s_qk23, 2 * (b + 1) + 1)
                    spread(1, 1 - r, s_qb23)
                    sp.wait_ge(s_nm, 2 * (b + 1) + 1)
                    maxima(0, 1 - r, s_nmA)
                if Q:
                    sp.wait_ge(s_qk01, 2 * (b + 2) + 1)
                    spread(0, r, s_qb01)
                if N:
                    if F:
                        sp.wait_ge(s_res, b)
                    residual(b + 1, 1 - r)
                if S:
                    for c, _ in finals(b):
                        store(c)

            def store(c):
                sp.wait_ge(s_fin, c + 1)
                sp.dma_start(ov[:, bass.ds(c * TT, TT), :], X[:, bass.ds(c * TT, TT), :]).then_inc(s_out, 16)

            def routed():
                sp.wait_ge(s_scat[0], 16 * TILES)
                sp.wait_ge(s_scat[1], 16 * TILES)
                sp.wait_ge(s_h, (ROUTED_AT + 2) * NC)
                for j in range(4):
                    sp.dma_start(xs[:, j, :], slots[j * P:j * P + P]).then_inc(s_xs[j], 16)

                def store_result(j, r):
                    sp.wait_ge(s_ys, j + 1)
                    sp.dma_start(results[bass.ds(j * P, P), :], ys[:, r, :]).then_inc(s_yst[r], 16)

                def load(j, q):
                    sp.wait_ge(s_xt, j - 3)
                    sp.dma_start(xs[:, q, :], slots[bass.ds(j * P, P), :]).then_inc(s_xs[q], 16)

                for j in range(4, 8):
                    load(j, j % 4)
                    if j == 7:
                        store_result(0, 0)
                with sp.Fori(1, NT // 4 - 1) as i:
                    for q in range(4):
                        load(i * 4 + (q + 4), q)
                        store_result(i * 4 + (q - 3), (q + 1) % 2)
                for j in range(NT - 7, NT):
                    store_result(j, j % 2)

            def after(b):
                if b == 0:
                    sp.wait_ge(s_tex, 2)
                    for e in range(LATE - 1, E):
                        sp.dma_start(Dn[:, e + 1], w_down[e].rearrange("(c p) d -> p c d", p=P)).then_inc(s_dn, 16)

            batches(body, sp, after=after, routed=routed)
            store(15)
            sp.wait_ge(s_out, 16 * B)

        @block.gpsimd
        def _(pool):
            nc.gpsimd.memset(ident[:], 0.0).then_inc(s_id, 1)
            nc.gpsimd.memset(V[:], 0.0).then_inc(s_vz, 1)
            pool.wait_ge(s_id, 1)
            nc.gpsimd.affine_select(out=ident[:], in_=ident[:], compare_op=ALU.not_equal, fill=1.0, base=0,
                                    pattern=[[-1, P]], channel_multiplier=1).then_inc(s_id, 1)
            nc.gpsimd.memset(Qb[:].bitcast(F32), 0.0).then_inc(s_qz, 1)
            pool.wait_ge(s_vz, 1)
            for r in range(2):
                for t in range(TT):
                    nc.gpsimd.memset(V[:, r, t, 0:NH * VW].rearrange("p (h c) -> p h c", c=VW)[:, :, HD:VW],
                                     1.0).then_inc(s_vz, 1)
            nc.gpsimd.memset(sel, 1.0).then_inc(s_sel, 1)
            pool.wait_ge(s_sel, 1)
            nc.gpsimd.affine_select(out=sel[:, 0, :], in_=sel[:, 0, :], compare_op=ALU.is_gt, fill=0.0, base=0,
                                    pattern=[[1, P]], channel_multiplier=-1).then_inc(s_sel, 1)
            nc.gpsimd.iota(thr[:], pattern=[[P, TILES]], base=0, channel_multiplier=0,
                           allow_small_or_imprecise_dtypes=True).then_inc(s_sel, 1)
            nc.gpsimd.iota(tix[:], pattern=[[1, NT]], base=0, channel_multiplier=0,
                           allow_small_or_imprecise_dtypes=True).then_inc(s_sel, 1)

            def fetch(b, r):
                nc.gpsimd.tensor_copy(xch[:, r, :], xTh[:, b * T:b * T + T].bitcast(F32)).then_inc(s_xc, 1)
                nc.gpsimd.tensor_copy(xcl[:, r, :], xTl[:, b * T:b * T + T].bitcast(F32)).then_inc(s_xc, 1)

            def add_bias(b, r):
                pool.wait_ge(s_xrl[r], 16 * (b // 2 + 1))
                x2 = xr[:, r, :].rearrange("p (t d) -> p t d", t=TT)
                nc.gpsimd.tensor_tensor(x2, x2, BVP[:, D:].unsqueeze(1).to_broadcast([P, TT, D]),
                                        ALU.add).then_inc(s_xrb, 1)

            def dispatch(tiles):
                for t in tiles:
                    r, n = t // TT % 2, t // TT // 2
                    if t % TT == 0 and n:
                        pool.wait_ge(s_scat[r], 64 * n)
                    for k in range(2):
                        pool.indirect_dma_start(
                            out=slots, out_offset=bass.IndirectOffsetOnAxis(ap=pos[:, k, t:t + 1], axis=0),
                            in_=X[:, t, :], in_offset=None).then_inc(s_scat[r], 16)

            def collect(c):
                if c >= 2:
                    pool.wait_ge(s_fin, c - 1)
                for k in range(2):
                    for t in range(TT):
                        pool.indirect_dma_start(
                            out=G[:, c % 2, k * TT + t, :], out_offset=None, in_=results,
                            in_offset=bass.IndirectOffsetOnAxis(ap=pos[:, k, c * TT + t:c * TT + t + 1], axis=0),
                        ).then_inc(s_G[c % 2], 16)

            pool.wait_ge(s_lo, 8)
            pool.wait_ge(s_hi, 8)
            pool.wait_ge(s_bias, 1)
            shares = {3: range(4, 8), 4: range(8, 16), 5: range(16, 24), 6: range(24, 32)}
            for b in range(B):
                if b >= 2:
                    pool.wait_ge(s_up, (b - 1) * NC)
                fetch(b, b % 2)
                if b == 3:
                    pool.wait_ge(s_pos, 2)
                    pool.wait_ge(s_zero, 32)
                    dispatch(range(0, 4))
                if 1 <= b < 9:
                    add_bias(b - 1, (b - 1) % 2)
                if b in shares:
                    dispatch(shares[b])
                if b == 9:
                    pool.wait_ge(s_yst[0], 8 * NT)
                    pool.wait_ge(s_yst[1], 8 * NT)
                    collect(0)
                    collect(1)
                if b >= 10:
                    collect(b - 8)
                if b >= 9:
                    add_bias(b - 1, (b - 1) % 2)
            for c in range(8, B):
                collect(c)
                if c == 11:
                    add_bias(B - 1, 1)

        @block.scalar
        def _(act):
            for e in range(FFNS):
                act.wait_ge(s_u[e % 2], 16 * (e // 2 + 1))
                nc.scalar.activation(Uh[:, e, :], ust[:, e % 2, :], ACT.Copy).then_inc(s_uh, 1)
            act.wait_ge(s_stat, 1)
            nc.scalar.activation(nrm[:, 1, :], nrm[:, 0, :], ACT.Sqrt).then_inc(s_sq, 1)
            for c in range(8):
                act.wait_ge(s_xnT, c + 1)
                nc.scalar.activation(xTh[:, 512 * c:512 * c + 512], sbank[c % 2][:], ACT.Copy).then_inc(s_hi, 1)
            act.wait_ge(s_lg, 1)
            nc.scalar.activation(table(0).rearrange("p t e -> p (t e)"), tbank[0][:, 0:TILES * E], ACT.Exp,
                                 scale=-1.0).then_inc(s_sig, 1)

            def ffn(b, k):
                if k in FILL and FILL[k][0] == "up":
                    n = FILL[k][1]
                    act.wait_ge(s_up, b * NC + n + 1)
                    wait(act, s_h, b * NC + n)
                    nc.scalar.activation(R[:], fbank[:], ACT.Relu).then_inc(s_r, 1)

            def partial(b, r, n, qk, produced, s_t, freed):
                act.wait_ge(produced, 2 * b + qk + 1)
                wait(act, freed[0], freed[1])
                for g in range(2):
                    ins = nc.scalar.activation(tmp[:, qk, g, :], pbank[:, g * T:g * T + T], ACT.Identity,
                                               bias=bias[:, 10 + 4 * qk + 2 * n + g:11 + 4 * qk + 2 * n + g],
                                               scale=bias[:, 8 + qk:9 + qk])
                ins.then_inc(s_t, 1)

            def keep_output(b, n):
                act.wait_ge(s_pv, b * 8 + 4 * n + 4)
                wait(act, s_tr, 2 * b + n - 1)
                nc.scalar.activation(OS[:, n], obank[:].rearrange("p (g q) -> p g q", g=2), ACT.Copy).then_inc(s_os, 1)

            def keep_maxima(b, n, loaded):
                act.wait_ge(s_mt, 2 * b + n + 1)
                wait(act, loaded, 64 * b)
                nc.scalar.activation(NM[:, n, :], wbank[0:8, 0:T], ACT.Copy).then_inc(s_nm, 1)

            def body(b, r, F, A, N, Q, S):
                for j in range(SLOTS):
                    for u in (2 * j, 2 * j + 1):
                        if A:
                            act.wait_ge(s_st, b * NU + u + 1)
                            wait(act, s_pv, b * 8 + j - 1)
                            nc.scalar.activation(PT[:, u % 4, :], tbank[u % 2][:], ACT.Exp, scale=SCALE).then_inc(s_e, 1)
                        if F and u == 0:
                            keep_output(b - 1, 1)
                        if A and u == 8:
                            keep_output(b, 0)
                    if N and j < 2:
                        partial(b + 1, 1 - r, 1, j, s_p23, s_t23, (s_qk01, 2 * (b + 1) + j + 1))
                    if Q and j in (4, 5):
                        partial(b + 2, r, 0, j - 4, s_p01, s_t01, (s_qk23, 2 * (b + 1) + j - 3))
                    if N:
                        ffn(b + 1, 2 * j)
                    if A and j == 0:
                        keep_maxima(b, 1, s_nmB)
                    if F and j == 3:
                        act.wait_ge(s_ant, b)
                        wait(act, s_y, b - 1)
                        nc.scalar.activation(AT[:], wbank[:, 0:T], ACT.Copy).then_inc(s_at, 1)
                    if N and j == 4:
                        keep_maxima(b + 1, 0, s_nmA)
                    if N:
                        ffn(b + 1, 2 * j + 1)

            def step(s, i, c):
                r = c % 2
                if within(s, 0):
                    act.wait_ge(s_xt, s + 1)
                    wait(act, s_hu, s - 1)
                    nc.scalar.activation(xrh[:, r, :], sbank[0][:, 0:P], ACT.Copy).then_inc(s_xh, 1)
                if within(s, 2):
                    act.wait_ge(s_ht, s - 1)
                    wait(act, s_yd, s - 3)
                    nc.scalar.activation(hr[:, r].rearrange("p c m -> p (c m)"), (wbank, fbank)[r][:],
                                         ACT.Square).then_inc(s_hr, 1)

            batches(body, act, routed=lambda: steps(step, act))

        @block.vector
        def _(dve):
            chain = [0]

            def link(ins):
                chain[0] += 1
                ins.then_inc(s_dve, 1)
                dve.wait_ge(s_dve, chain[0])

            for k in range(4):
                dve.wait_ge(s_w[k], 16)
            link(nc.vector.tensor_copy(wsh[:], wst[:]))
            nc.vector.memset(Wqh[:].bitcast(F32), 0.0)
            nc.vector.memset(Wql[:].bitcast(F32), 0.0)
            nc.vector.memset(rows[0:1, 512:2048], 0.0)
            nc.vector.memset(bias[:], 0.0)
            nc.vector.tensor_tensor(wsl[:], wst[:], wsh[:].bitcast(F32), ALU.subtract)
            link(nc.vector.tensor_copy(Wrh[:], Wr[:]))
            nc.vector.tensor_tensor(Wrl[:], Wr[:], Wrh[:].bitcast(F32), ALU.subtract).then_inc(s_wr, 1)
            for qk in range(2):
                for src, dst in ((wsh, Wqh), (wsl, Wql)):
                    for p in PART:
                        o = dst[:, qk].rearrange("p g (q c) -> p (g q) c", c=32)[:, :, p:p + 8]
                        i = src[:, qk * D:(qk + 1) * D].bitcast(F32).rearrange("p (h d) -> p h d", d=HD)
                        nc.vector.tensor_copy(o, i)
                for p in PART:
                    o = rows[0:1, 512 + 512 * qk:1024 + 512 * qk].rearrange("p (h c) -> p h c", c=32)[:, :, p:p + 8]
                    nc.vector.tensor_copy(o, rows[0:1, qk * D:(qk + 1) * D].rearrange("p (h d) -> p h d", d=HD))
                p = PART[(QLO, KLO)[qk]]
                m = rows[0:1, 1536 + P * qk:1536 + P * qk + P].rearrange("p (q c) -> p q c", c=32)
                nc.vector.memset(m[:, :, p:p + 8], 1.0)
            nc.vector.memset(rows[0:1, 1024:1536].rearrange("p (h c) -> p h c", c=32)[:, :, 0:1], 1.0)
            nc.vector.memset(rows[0:1, 1792:1920], 1.0).then_inc(s_rows, 1)
            for c in range(4):
                dve.wait_ge(s_x[c], 16)
                for t in range(8 * c, 8 * c + 8):
                    nc.vector.bn_stats(st6[:, t, :], X[:, t, :]).then_inc(s_dve, 1)
            chain[0] += TILES
            dve.wait_ge(s_dve, chain[0])
            for t in range(TILES):
                nc.vector.bn_aggr(mv[:, t, :], st6[:, t, :]).then_inc(s_dve, 1)
            chain[0] += TILES
            dve.wait_ge(s_dve, chain[0])
            nc.vector.tensor_scalar(nrm[:, 0, :], mv[:, :, 1], EPS, None, ALU.add).then_inc(s_stat, 1)
            for e in range(FFNS):
                dve.wait_ge(s_uh, e + 1)
                nc.vector.tensor_tensor(Ul[:, e, :], ust[:, e % 2, :], Uh[:, e, :].bitcast(F32), ALU.subtract).then_inc(s_ul, 1)
            dve.wait_ge(s_sq, 1)
            link(nc.vector.reciprocal(nrm[:, 2, :], nrm[:, 1, :]))
            link(nc.vector.tensor_tensor(nrm[:, 3, :], nrm[:, 2, :], nrm[:, 2, :], ALU.mult))
            link(nc.vector.tensor_tensor(nrm[:, 3, :], nrm[:, 3, :], nrm[:, 0, :], ALU.mult))
            link(nc.vector.tensor_scalar(nrm[:, 3, :], nrm[:, 3, :], -0.5, 1.5, ALU.mult, ALU.add))
            link(nc.vector.tensor_tensor(nrm[:, 1, :], nrm[:, 3, :], nrm[:, 2, :], ALU.mult))
            dve.wait_ge(s_bps, 1)
            link(nc.vector.tensor_copy(bias[:, 0:10], wbank[:, 0:10]))
            for qk in range(2):
                nc.vector.tensor_scalar(bias[:, 10 + 4 * qk:14 + 4 * qk], bias[:, 4 * qk:4 * qk + 4],
                                        bias[:, 8 + qk:9 + qk], None, ALU.mult)
            nc.vector.tensor_copy(BVP[:], wbank[:, 128:384]).then_inc(s_bias, 1)

            def low_part(c):
                dve.wait_ge(s_hi, c + 1)
                cols = slice(512 * c, 512 * c + 512)
                nc.vector.tensor_tensor(xTl[:, cols], sbank[c % 2][:], xTh[:, cols].bitcast(F32),
                                        ALU.subtract).then_inc(s_lo, 1)

            for c in range(8):
                for t in range(CHUNK * c, CHUNK * c + CHUNK):
                    ins = nc.vector.tensor_scalar(X[:, t, :], X[:, t, :], mv[:, t, 0:1], nrm[:, 1, t:t + 1],
                                                  ALU.subtract, ALU.mult)
                ins.then_inc(s_xn, 1)
                if c:
                    low_part(c - 1)
            low_part(7)
            Xf = X[:].rearrange("p t d -> p (t d)")

            def bc(ap):
                return ap.unsqueeze(2).to_broadcast([P, TILES, E])

            def choose():
                for e in range(E):
                    nc.vector.memset(wte[:, e:e + 1], float(E - e))
                dve.wait_ge(s_sig, 1)
                p, work, rest = table(0), table(3), table(4)
                wt = wte[:].unsqueeze(1).to_broadcast([P, TILES, E])
                link(nc.vector.tensor_scalar(p, p, 1.0, None, ALU.add))
                link(nc.vector.reciprocal(p, p))
                src = p
                for k in range(2):
                    link(nc.vector.tensor_reduce(rm[:, k, :], src, AX_X, ALU.max))
                    link(nc.vector.tensor_tensor(work, src, bc(rm[:, k, :]), ALU.is_equal))
                    link(nc.vector.tensor_tensor(work, work, wt, ALU.mult))
                    link(nc.vector.tensor_reduce(rm[:, 2, :], work, AX_X, ALU.max))
                    link(nc.vector.tensor_tensor(table(1 + k), work, bc(rm[:, 2, :]), ALU.is_equal))
                    if k == 0:
                        link(nc.vector.tensor_scalar(rest, table(1), -2.0, None, ALU.mult))
                        link(nc.vector.tensor_tensor(rest, rest, p, ALU.add))
                        src = rest
                nc.vector.tensor_tensor(table(5), table(1), table(2), ALU.add).then_inc(s_M, 1)
                link(nc.vector.tensor_tensor(rm[:, 2, :], rm[:, 0, :], rm[:, 1, :], ALU.add))
                link(nc.vector.tensor_scalar(rm[:, 2, :], rm[:, 2, :], 1e-6, None, ALU.add))
                link(nc.vector.reciprocal(rm[:, 3, :], rm[:, 2, :]))
                for k in range(2):
                    link(nc.vector.tensor_tensor(rm[:, k, :], rm[:, k, :], rm[:, 3, :], ALU.mult))

            def place():
                dve.wait_ge(s_cnt, 1)
                before, total, run, tmp_, at = table(6), table(7), table(3), table(4), table(0)
                half = TILES * E
                nc.vector.memset(cnt[:, 4, :], 0.0)
                nc.vector.tensor_copy(before.rearrange("p t e -> p (t e)"), fbank[:, 0:half]).then_inc(s_cntr, 1)
                nc.vector.tensor_copy(total.rearrange("p t e -> p (t e)"), fbank[:, half:2 * half]).then_inc(s_cntr, 1)
                dve.wait_ge(s_cntr, 2)
                a, o = total, run
                step = 1
                while step < TILES:
                    nc.vector.tensor_copy(o[:, 0:step], a[:, 0:step])
                    link(nc.vector.tensor_tensor(o[:, step:], a[:, step:], a[:, 0:TILES - step], ALU.add))
                    a, o = o, (tmp_ if o is run else run)
                    step *= 2
                cmp = at.rearrange("p t e -> p (t e)").rearrange("p (e t) -> p e t", e=E)
                link(nc.vector.tensor_tensor(cmp, a[:, TILES - 1, :].unsqueeze(2).to_broadcast([P, E, TILES]),
                                             thr[:].unsqueeze(1).to_broadcast([P, E, TILES]), ALU.is_gt))
                link(nc.vector.tensor_reduce(cnt[:, 0, :], cmp, AX_X, ALU.add))
                c, d = 0, 1
                step = 1
                while step < E:
                    nc.vector.tensor_copy(cnt[:, d, 0:step], cnt[:, c, 0:step])
                    link(nc.vector.tensor_tensor(cnt[:, d, step:], cnt[:, c, step:], cnt[:, c, 0:E - step], ALU.add))
                    c, d = d, d + 1
                    step *= 2
                ends = cnt[:, c, :]
                link(nc.vector.tensor_scalar(cnt[:, 4, 1:E], ends[:, 0:E - 1], float(P), None, ALU.mult))
                link(nc.vector.tensor_tensor(at[:, 1:], before[:, 1:], a[:, 0:TILES - 1], ALU.add))
                link(nc.vector.tensor_copy(at[:, 0:1], before[:, 0:1]))
                link(nc.vector.tensor_tensor(at, at, cnt[:, 4, :].unsqueeze(1).to_broadcast([P, TILES, E]), ALU.add))
                for k in range(2):
                    link(nc.vector.tensor_tensor(before, at, table(1 + k), ALU.mult))
                    link(nc.vector.tensor_reduce(rm[:, 2, :], before, AX_X, ALU.add))
                    nc.vector.tensor_copy(pos[:, k, :], rm[:, 2, :]).then_inc(s_pos, 1)
                    dve.wait_ge(s_pos, k + 1)
                nc.vector.memset(tex[:], 0.0).then_inc(s_tex, 1)
                dve.wait_ge(s_tex, 1)
                for e in range(E - 1):
                    link(nc.vector.scalar_tensor_tensor(out=tex[:], in0=tix[:], scalar=ends[0:1, e:e + 1],
                                                        in1=tex[:], op0=ALU.is_ge, op1=ALU.add))
                nc.vector.tensor_copy(texi[:], tex[:]).then_inc(s_tex, 1)

            def ffn(b, k, q):
                if k not in FILL:
                    return
                kind, n = FILL[k]
                if kind == "up":
                    dve.wait_ge(s_r, b * NC + n + 1)
                    wait(dve, s_dwn, b)
                    nc.vector.tensor_tensor(hT[:, 2 * n:2 * n + 2, :].rearrange("p c m -> p (c m)"), R[:], R[:],
                                            ALU.mult).then_inc(s_h, 1)
                else:
                    dve.wait_ge(s_dwn, b + 1)
                    dve.wait_ge(s_xrb, b + 1)
                    y = xr[:, q, :]
                    nc.vector.tensor_tensor(y, fbank[:, 0:T], y, ALU.add).then_inc(s_cmb, 1)

            def split(b, r, n, qk, s_t, done):
                dve.wait_ge(s_t, 2 * b + qk + 1)
                if qk == 0:
                    wait(dve, (s_qb01, s_qb23)[n], 64 * b)
                for g in range(2):
                    dst = Qd[:, 2 * n + g, :] if qk == 0 else Kd[:, r, 2 * n + g, :]
                    ins = nc.vector.scalar_tensor_tensor(
                        out=dst, in0=pbank[:, g * T:g * T + T], scalar=bias[:, 4 * qk + 2 * n + g:4 * qk + 2 * n + g + 1],
                        in1=tmp[:, qk, g, :].bitcast(F32), op0=ALU.add, op1=ALU.subtract)
                ins.then_inc(done, 1)

            def normalise(b, n):
                dve.wait_ge(s_tr, 2 * b + n + 1)
                wait(dve, s_ant, b)
                m = wbank[:].rearrange("p (q h c) -> p q h c", q=TT, c=32)
                nc.vector.reciprocal(rs[:, n, :].rearrange("p (q h c) -> p q h c", q=TT, c=1), m[:, :, :, 8:9]).then_inc(s_rs, 1)
                dve.wait_ge(s_rs, 2 * b + n + 1)
                nc.vector.tensor_tensor(
                    AN[:, :, 64 * n:64 * n + 64].rearrange("p q (h d) -> p q h d", d=HD), m[:, :, :, 0:8],
                    rs[:, n, :].rearrange("p (q h) -> p q h", q=TT).unsqueeze(3).to_broadcast([P, TT, 8, HD]),
                    ALU.mult).then_inc(s_nrm, 1)

            def body(b, r, F, A, N, Q, S):
                for j in range(SLOTS):
                    for h in (2 * j, 2 * j + 1):
                        if N:
                            dve.wait_ge(s_s, (b + 1) * NU + h + 1)
                            wait(dve, s_mt, 2 * b + 1 + h // 8)
                            nc.vector.tensor_reduce(Mx[:, h // 8, :, h % 4, (h // 4) % 2],
                                                    sbank[h % 2][:].rearrange("p (q k) -> p q k", q=TT), AX_X, ALU.max,
                                                    negate=True).then_inc(s_mx, 1)
                    if N and j < 2:
                        split(b + 1, 1 - r, 1, j, s_t23, s_qk23)
                    if N and j == 2:
                        dve.wait_ge(s_vps, b + 2)
                        nc.vector.tensor_tensor(
                            V[:, 1 - r, :, 0:NH * VW].rearrange("p t (h c) -> p t h c", c=VW)[:, :, :, 0:HD],
                            pbank[:, 0:2 * D].rearrange("p (t h d) -> p t h d", t=TT, d=HD),
                            BVP[:, 0:D].rearrange("p (h d) -> p h d", d=HD).unsqueeze(1).to_broadcast([P, TT, NH, HD]),
                            ALU.add).then_inc(s_v, 1)
                    if Q and j in (4, 5):
                        split(b + 2, r, 0, j - 4, s_t01, s_qk01)
                    if N:
                        ffn(b + 1, 2 * j, 1 - r)
                    if F and j == 1:
                        normalise(b - 1, 1)
                    if F and j == 5:
                        dve.wait_ge(s_y, b)
                        dve.wait_ge(s_cmb, b)
                        dve.wait_ge(s_scat[1 - r], (b - 1 - (1 - r)) * 32 + 64)
                        nc.vector.tensor_tensor(Xf[:, bass.ds((b - 1) * TT * D, TT * D)], wbank[:, 0:T],
                                                xr[:, 1 - r, :], ALU.add).then_inc(s_res, 1)
                    if A and j == 6:
                        normalise(b, 0)
                    if S:
                        for c, at in finals(b):
                            if at == j:
                                finish(c, c % 2 if isinstance(c, int) else 1 - r)
                    if N:
                        ffn(b + 1, 2 * j + 1, 1 - r)

            def finish(c, q):
                dve.wait_ge(s_res, c + 1)
                dve.wait_ge(s_G[q], (c // 2 + 1) * 64 if isinstance(c, int) else (c - (0, 1)[q]) * 32 + 64)
                for k in range(2):
                    for t in range(TT):
                        o = Xf[:, bass.ds((c * TT + t) * D, D)]
                        w = rm[:, k, bass.ds(c * TT + t, 1)]
                        ins = nc.vector.scalar_tensor_tensor(out=o, in0=G[:, q, k * TT + t, :], scalar=w, in1=o,
                                                             op0=ALU.mult, op1=ALU.add)
                        if k == 0:
                            ins.then_inc(s_f0, 1)
                    if k == 0:
                        dve.wait_ge(s_f0, (c + 1) * TT)
                ins.then_inc(s_fin, 1)

            def after(b):
                if b == -1:
                    choose()
                if b == 0:
                    place()

            def step(s, i, c):
                r = c % 2
                if within(s, 0):
                    dve.wait_ge(s_xh, s + 1)
                    nc.vector.tensor_tensor(xrl[:, r, :], sbank[0][:, 0:P], xrh[:, r, :].bitcast(F32),
                                            ALU.subtract).then_inc(s_xl, 1)
                if within(s, 1):
                    dve.wait_ge(s_hu, s)
                    wait(dve, s_ht, s - 2)
                    nc.vector.tensor_scalar(rr[:, 1 - r, :], tbank[1 - r][:], 0.0, None, ALU.max).then_inc(s_rr, 1)
                if within(s, 3):
                    dve.wait_ge(s_yd, s - 2)
                    wait(dve, s_yst[1 - r], i * 32 + (c - 3) // 2 * 16)
                    nc.vector.tensor_copy(ys[:, 1 - r, :], (pbank, sbank[1])[1 - r][:, 0:D]).then_inc(s_ys, 1)

            batches(body, dve, after=after, routed=lambda: steps(step, dve))
            finish(15, 1)

        @block.tensor
        def _(pe):
            pe.wait_ge(s_rows, 1)
            one = rows[0:1, 1792:1793]
            for qk in range(2):
                for g in range(GROUPS):
                    a = 512 + 512 * qk + P * g
                    nc.tensor.matmul(wbank[:, 4 * qk + g:4 * qk + g + 1], rows[0:1, a:a + P], one, start=True, stop=True)
                a = 1536 + P * qk
                nc.tensor.matmul(wbank[:, 8 + qk:9 + qk], rows[0:1, a:a + P], one, start=True, stop=True)
            nc.tensor.matmul(wbank[:, 128:384], rows[0:1, 1792:1920], rows[0:1, 256:512],
                             start=True, stop=True).then_inc(s_bps, 1)
            pe.wait_ge(s_id, 2)
            for c in range(8):
                pe.wait_ge(s_xn, c + 1)
                if c >= 2:
                    pe.wait_ge(s_lo, c - 1)
                for t in range(CHUNK):
                    ins = nc.tensor.transpose(sbank[c % 2][:, t * P:t * P + P], X[:, CHUNK * c + t, :], ident[:])
                ins.then_inc(s_xnT, 1)
            def three(o, lh, ll, rh, rl):
                nc.tensor.matmul(o, lh, rl, start=True, stop=False)
                nc.tensor.matmul(o, ll, rh, start=False, stop=False)
                return nc.tensor.matmul(o, lh, rh, start=False, stop=True)

            pe.wait_ge(s_wr, 1)
            for c in range(8):
                pe.wait_ge(s_lo, c + 1)
                for t in range(CHUNK * c, CHUNK * c + CHUNK):
                    o = tbank[0][:, t * E:t * E + E]
                    cols = slice(t * P, t * P + P)
                    nc.tensor.matmul(o, xTl[:, cols], Wrh[:], start=True, stop=False)
                    nc.tensor.matmul(o, xTh[:, cols], Wrl[:], start=False, stop=False)
                    ins = nc.tensor.matmul(o, xTh[:, cols], Wrh[:], start=False, stop=True)
            ins.then_inc(s_lg, 1)
            pe.wait_ge(s_bias, 1)
            pe.wait_ge(s_vz, 5)
            pe.wait_ge(s_zero, 32)
            pe.wait_ge(s_sig, 1)
            pe.wait_ge(s_w[4], 16)
            pe.wait_ge(s_ul, 1)
            pe.wait_ge(s_dn0, 16)

            def count():
                pe.wait_ge(s_M, 1)
                pe.wait_ge(s_sel, 4)
                pe.wait_ge(s_cmb, 2)
                for k in range(2):
                    ins = nc.tensor.matmul(fbank[:, k * TILES * E:(k + 1) * TILES * E], sel[:, k, :],
                                           table(5).rearrange("p t e -> p (t e)"), start=True, stop=True)
                ins.then_inc(s_cnt, 1)

            def ffn(b, k, q):
                if k not in FILL:
                    return
                kind, n = FILL[k]
                if kind == "up":
                    wait(pe, s_r, b * NC + n)
                    if n == 0:
                        wait(pe, s_cmb, b)
                        if isinstance(b, int) and b == 2:
                            pe.wait_ge(s_cntr, 2)
                    for c in range(2):
                        w = slice((2 * n + c) * P, (2 * n + c + 1) * P)
                        ins = three(fbank[:, c * T:c * T + T], Uh[:, 0, w], Ul[:, 0, w], xch[:, q, :], xcl[:, q, :])
                    ins.then_inc(s_up, 1)
                else:
                    pe.wait_ge(s_h, b * NC + 2)
                    for t in range(TT):
                        for c in range(HC):
                            ins = nc.tensor.matmul(fbank[:, t * D:t * D + D], hT[:, c, t * P:t * P + P],
                                                   Dn[:, 0, c, :], start=c == 0, stop=c == HC - 1)
                    ins.then_inc(s_dwn, 1)

            def project(b, r, n, qk, done):
                wait(pe, s_xc, 2 * (b + 1))
                for g in range(2):
                    w = 2 * n + g
                    ins = three(pbank[:, g * T:g * T + T], Wqh[:, qk, w, :], Wql[:, qk, w, :], xch[:, r, :], xcl[:, r, :])
                ins.then_inc(done, 1)

            def turn(b, n):
                pe.wait_ge(s_os, 2 * b + n + 1)
                for t in range(TT):
                    for g in range(2):
                        ins = nc.tensor.transpose(wbank[:, (2 * t + g) * P:(2 * t + g) * P + P],
                                                  OS[:, n, g, t * P:t * P + P], ident[:])
                ins.then_inc(s_tr, 1)

            def turn_max(b, n):
                pe.wait_ge(s_mx, b * NU + 8 * n + 8)
                for t in range(TT):
                    ins = nc.tensor.transpose(wbank[0:8, t * P:t * P + P],
                                              Mx[:, n, t].rearrange("p q g -> p (q g)"), ident[:])
                ins.then_inc(s_mt, 1)

            def body(b, r, F, A, N, Q, S):
                for j in range(SLOTS):
                    if A:
                        if j == 0:
                            pe.wait_ge(s_nmA, 64 * (b + 1))
                        if j == 4:
                            pe.wait_ge(s_nmB, 64 * (b + 1))
                        for u in (2 * j, 2 * j + 1):
                            g, kt, half = u // 4, (u // 2) % 2, u % 2
                            wait(pe, s_e, b * NU + u - 1)
                            nc.tensor.matmul(tbank[u % 2][:], Kd[:, r, g, kt * P:kt * P + P],
                                             Qb[:, r, g, 2 * half:2 * half + 2, :], start=True, stop=True).then_inc(s_st, 1)
                    if N and j == 0:
                        wait(pe, s_qk01, 2 * (b + 1) + 2)
                        project(b + 1, 1 - r, 1, 0, s_p23)
                    if N and j == 1:
                        pe.wait_ge(s_qk23, 2 * (b + 1) + 1)
                        project(b + 1, 1 - r, 1, 1, s_p23)
                    if N and j == 2:
                        pe.wait_ge(s_qk23, 2 * (b + 1) + 2)
                        for t in range(TT):
                            ins = three(pbank[:, t * D:t * D + D], xch[:, 1 - r, t * P:t * P + P],
                                        xcl[:, 1 - r, t * P:t * P + P], wsh[:, 2 * D:], wsl[:, 2 * D:])
                        ins.then_inc(s_vps, 1)
                    if Q and j == 4:
                        if N:
                            pe.wait_ge(s_v, b + 2)
                        project(b + 2, r, 0, 0, s_p01)
                    if Q and j == 5:
                        pe.wait_ge(s_qk01, 2 * (b + 2) + 1)
                        project(b + 2, r, 0, 1, s_p01)
                    for h in (2 * j, 2 * j + 1):
                        if N:
                            g, q = h // 4, h % 4
                            if h == 0:
                                pe.wait_ge(s_qk01, 2 * (b + 1) + 2)
                                pe.wait_ge(s_qb01, 64 * (b + 2))
                            if h == 8:
                                pe.wait_ge(s_qk23, 2 * (b + 1) + 2)
                                pe.wait_ge(s_qb23, 64 * (b + 2))
                            wait(pe, s_mx, (b + 1) * NU + h - 1)
                            for t in range(TT):
                                ins = nc.tensor.matmul(sbank[h % 2][:, t * T:t * T + T],
                                                       Qb[:, 1 - r, g, q, t * P:t * P + P], Kd[:, 1 - r, g, :],
                                                       start=True, stop=True)
                            ins.then_inc(s_s, 1)
                        if N and h % 2 == 0:
                            ffn(b + 1, h, 1 - r)
                    if A and j == 0:
                        pe.wait_ge(s_nm, 2 * b + 1)
                        wait(pe, s_nrm, 2 * b - 1)
                        turn_max(b, 1)
                    if F and j == 1:
                        if A:
                            pe.wait_ge(s_nm, 2 * b + 2)
                        else:
                            pe.wait_ge(s_nrm, 2 * b - 1)
                        turn(b - 1, 1)
                    if F and j == 3:
                        pe.wait_ge(s_nrm, 2 * b)
                        for t in range(TT):
                            ins = nc.tensor.transpose(wbank[:, t * P:t * P + P], AN[:, t, :], ident[:])
                        ins.then_inc(s_ant, 1)
                    if N and j == 4:
                        if F:
                            pe.wait_ge(s_at, b)
                        elif A:
                            pe.wait_ge(s_nm, 2 * b + 2)
                        turn_max(b + 1, 0)
                    if F and j == 5:
                        pe.wait_ge(s_at, b)
                        if N:
                            pe.wait_ge(s_nm, 2 * b + 3)
                        for t in range(TT):
                            ins = nc.tensor.matmul(wbank[:, t * D:t * D + D], AT[:, t * P:t * P + P], Wp[:],
                                                   start=True, stop=True)
                        ins.then_inc(s_y, 1)
                    if A and j == 6:
                        if F:
                            pe.wait_ge(s_res, b)
                        elif N:
                            pe.wait_ge(s_nm, 2 * b + 3)
                        turn(b, 0)
                    if A:
                        g, kt = j // 2, j % 2
                        pe.wait_ge(s_e, b * NU + 2 * j + 2)
                        if j == 0:
                            pe.wait_ge(s_v, b + 1)
                            wait(pe, s_os, 2 * b)
                        if j == 4:
                            pe.wait_ge(s_os, 2 * b + 1)
                        for q in range(LANES):
                            ins = nc.tensor.matmul(obank[32 * q:32 * q + 32, (g % 2) * T:(g % 2) * T + T],
                                                   V[:, r, kt, (4 * g + q) * VW:(4 * g + q) * VW + 32],
                                                   PT[:, (2 * j + q // 2) % 4, (q % 2) * T:(q % 2) * T + T],
                                                   start=kt == 0, stop=kt == 1)
                        ins.then_inc(s_pv, 1)
                    if N:
                        ffn(b + 1, 2 * j + 1, 1 - r)

            def expert(j):
                return pe.value_load(texi[0:1, bass.ds(j, 1)], min_val=0, max_val=E - 1)

            Uhf, Ulf = (w[:].rearrange("p e h -> p (e h)") for w in (Uh, Ul))
            Dnf = Dn[:].rearrange("p e c d -> p (e c d)")

            def step(s, i, c):
                r = c % 2
                if within(s, 0):
                    pe.wait_ge(s_xs[c % 4], i * 16 + (c // 4 + 1) * 16)
                    wait(pe, s_xl, s)
                    nc.tensor.transpose(sbank[0][:, 0:P], xs[:, c % 4, :], ident[:]).then_inc(s_xt, 1)
                if within(s, 3):
                    j, q = s - 3, 1 - r
                    e = expert(j)
                    pe.wait_ge(s_hr, j + 1)
                    wait(pe, s_ys, j - 1)
                    for k in range(HC):
                        ins = nc.tensor.matmul((pbank, sbank[1])[q][:, 0:D], hr[:, q, k, :],
                                               Dnf[:, bass.ds((e + 1) * H + k * D, D)], start=k == 0, stop=k == HC - 1)
                    ins.then_inc(s_yd, 1)
                if within(s, 2):
                    j = s - 2
                    pe.wait_ge(s_rr, j + 1)
                    wait(pe, s_hr, j - 1)
                    for k in range(HC):
                        ins = nc.tensor.transpose((wbank, fbank)[r][:, k * P:k * P + P], rr[:, r, k * P:k * P + P], ident[:])
                    ins.then_inc(s_ht, 1)
                if within(s, 1):
                    j, q = s - 1, 1 - r
                    e = expert(j)
                    pe.wait_ge(s_xl, j + 1)
                    wait(pe, s_rr, j - 1)
                    cols = bass.ds((e + 1) * H, H)
                    three(tbank[q][:], xrh[:, q, :], xrl[:, q, :], Uhf[:, cols], Ulf[:, cols]).then_inc(s_hu, 1)

            def routed():
                pe.wait_ge(s_mx, (ROUTED_AT + 2) * NU)
                pe.wait_ge(s_e, (ROUTED_AT + 1) * NU)
                pe.wait_ge(s_qk01, 2 * (ROUTED_AT + 2) + 2)
                pe.wait_ge(s_nrm, 2 * ROUTED_AT + 1)
                pe.wait_ge(s_r, (ROUTED_AT + 2) * NC)
                pe.wait_ge(s_cmb, ROUTED_AT + 2)
                pe.wait_ge(s_tex, 2)
                pe.wait_ge(s_ul, FFNS)
                pe.wait_ge(s_dn, 16 * E)
                steps(step, pe)
                pe.wait_ge(s_ys, NT)

            batches(body, pe, after=lambda b: count() if b == 0 else None, routed=routed)


def kernel(L0_attn_x, L0_attn_qkv_w, L0_attn_qkv_b, L0_attn_proj_w, L0_attn_proj_b, L0_ffn_W_router,
           L0_ffn_W_up, L0_ffn_W_down, L0_ffn_W_sh_up, L0_ffn_W_sh_down):
    import numpy as np
    import concourse.bacc as bacc
    from concourse.bass_utils import run_bass_kernel_spmd

    nc = bacc.Bacc("TRN2", target_bir_lowering=False, num_devices=1)
    given = {
        "x": L0_attn_x, "wqkvT": np.transpose(L0_attn_qkv_w), "bqkv": np.reshape(L0_attn_qkv_b, (1, -1)),
        "wprojT": np.transpose(L0_attn_proj_w), "bproj": np.reshape(L0_attn_proj_b, (1, -1)),
        "w_router": L0_ffn_W_router, "w_up": L0_ffn_W_up, "w_down": L0_ffn_W_down,
        "w_sup": L0_ffn_W_sh_up, "w_sdown": L0_ffn_W_sh_down,
    }
    arrays = {f"in_{k}": np.ascontiguousarray(v) for k, v in given.items()}
    args = [nc.dram_tensor(n, a.shape, F32, kind="ExternalInput").ap() for n, a in arrays.items()]
    out = nc.dram_tensor("out_0", (B, T, D), F32, kind="ExternalOutput").ap()
    slots = nc.dram_tensor("slots", (NT * P, D), F32, kind="Internal").ap()
    results = nc.dram_tensor("results", (NT * P, D), F32, kind="Internal").ap()
    build(nc, *args, slots, results, out)
    return run_bass_kernel_spmd(nc, [arrays], core_ids=[0]).results[0]["out_0"]
```

```python
from contextlib import ExitStack

import concourse.bass as bass
from concourse import mybir

F32 = mybir.dt.float32
F32R = mybir.dt.float32r
I32 = mybir.dt.int32
ALU = mybir.AluOpType
ACT = mybir.ActivationFunctionType
AX_X = mybir.AxisListType.X

P = 128
B, T, D = 16, 256, 128
NH, HD = 16, 8
GROUPS, LANES = 4, 4
TT = T // P
TILES = B * TT
E, H = 8, 512
HC = H // P
FFNS = E + 1
SCALE = HD ** -0.5
EPS = 1e-5
SLOTS = 8
VW = HD + 1
CHUNK = 4
CHUNKS = TILES // CHUNK
POOLED = 4
PART = [8, 16, 24]
LOW = (1, 2)

NU = 16
NC = 2
NT = TILES * 2 + E
PAIRS = NT // 2
LATE = FFNS - 4
ROUTED_AT = 6
FILL = {3: ("up", 0), 10: ("up", 1), 15: ("down", 0)}
PREPARE = {(-2, 5): 1, (-2, 6): 2, (-2, 7): 3, (-1, 0): 4, (-1, 2): 5, (-1, 4): 6, (-1, 6): 7}
FINAL = {13: ((12, 5),), 14: ((13, 5),), 15: ((14, 5),), 16: ((15, 5),)}


def build(nc, x, wqkvT, bqkv, wprojT, bproj, w_router, w_up, w_down, w_sup, w_sdown, slots, results, out):
    with ExitStack() as ctx:
        def sb(name, shape, dt=F32):
            return ctx.enter_context(nc.sbuf_tensor(name, shape, dt))

        def bank(name):
            return ctx.enter_context(nc.psum_tensor(name, [P, 512], F32))

        def sem(name):
            return ctx.enter_context(nc.semaphore(name))

        X = sb("X", [P, TILES, D])
        xT_hi = sb("xT_hi", [P, B * T], F32R)
        xT_lo = sb("xT_lo", [P, B * T], F32R)
        up_hi = sb("up_hi", [P, FFNS, H], F32R)
        up_lo = sb("up_lo", [P, FFNS, H], F32R)
        down_w = sb("down_w", [P, FFNS, HC, D])
        wqk_hi = sb("wqk_hi", [P, 2, GROUPS, P], F32R)
        wqk_lo = sb("wqk_lo", [P, 2, GROUPS, P], F32R)
        wqkv_hi = sb("wqkv_hi", [P, 3 * D], F32R)
        wqkv_lo = sb("wqkv_lo", [P, 3 * D], F32R)
        wproj = sb("wproj", [P, D])
        wrouter = sb("wrouter", [P, E])
        ident = sb("ident", [P, P])
        zeros = sb("zeros", [P, D])
        spare = sb("spare", [P, H])
        bias = sb("bias", [P, 20])
        bias_rows = sb("bias_rows", [P, 2 * D])
        stats = sb("stats", [P, TILES, 6])
        mean_var = sb("mean_var", [P, TILES, 2])
        norms = sb("norms", [P, 4, TILES])
        chosen_rows = sb("chosen_rows", [P, 4, TILES])
        rank = sb("rank", [P, E])
        tile_counts = sb("tile_counts", [P, 6, E])
        tile_starts = sb("tile_starts", [P, TILES])
        tile_index = sb("tile_index", [1, NT])
        tile_expert = sb("tile_expert", [1, NT])
        tile_weights = sb("tile_weights", [1, NT], I32)
        place_of = sb("place_of", [P, 2, TILES], I32)
        wrouter_hi = sb("wrouter_hi", [P, E], F32R)
        wrouter_lo = sb("wrouter_lo", [P, E], F32R)
        pair_hi = sb("pair_hi", [P, 2, P], F32R)
        pair_lo = sb("pair_lo", [P, 2, P], F32R)
        gathered = sb("gathered", [P, 2, 2 * TT, D])
        xb_hi = sb("xb_hi", [P, 2, T], F32R)
        xb_lo = sb("xb_lo", [P, 2, T], F32R)
        resid = sb("resid", [P, 2, TT * D])
        q_dense = sb("q_dense", [P, GROUPS, T], F32R)
        taken = sb("taken", [P, 2, 2, T], F32R)
        k_parts = sb("k_parts", [P, 2, GROUPS, T], F32R)
        q_blocks = sb("q_blocks", [P, 2, GROUPS, LANES, T], F32R)
        v_ones = sb("v_ones", [P, 2, TT, NH * VW + 32 - VW + 1])
        probs = sb("probs", [P, 4, 512])
        maxes = sb("maxes", [P, 2, TT, LANES, 2])
        max_rows = sb("max_rows", [8, 2, T], F32R)
        out_raw = sb("out_raw", [P, 2, 2, T])
        recips = sb("recips", [P, 2, 2 * TT * LANES])
        attn = sb("attn", [P, TT, D])
        attn_T = sb("attn_T", [P, T])
        relu_T = sb("relu_T", [P, 2 * T])
        hidden_T = sb("hidden_T", [P, HC, T])

        rows = probs[0:1].rearrange("p a b -> p (a b)")
        sel = gathered[:, 0, 0:2, :]
        raw = (gathered[:, 1].rearrange("p a d -> p (a d)"), spare)
        rawsh = out_raw[:, 0].rearrange("p g t -> p (g t)")
        wst = gathered[:, 1].rearrange("p a d -> p (a d)")[:, 0:3 * D]
        xs = [a.rearrange("p (k d) -> p k d", d=D)[:, 2 * k:2 * k + 2]
              for a in (relu_T[:], hidden_T[:, 0:2].rearrange("p c t -> p (c t)")) for k in range(2)]
        rr = out_raw[:].rearrange("p n g t -> p n (g t)")
        hr = probs[:, 0:2, :].rearrange("p k (c m) -> p k c m", c=HC)
        ys = gathered[:, 0]

        def table(k):
            w = TILES * E
            return down_w[:, LATE:].rearrange("p e c d -> p (e c d)")[:, k * w:k * w + w].rearrange("p (t e) -> p t e", e=E)

        sbank = [bank("sbank0"), bank("sbank1")]
        tbank = [bank("tbank0"), bank("tbank1")]
        obank = bank("obank")
        pbank = bank("pbank")
        wbank = bank("wbank")
        fbank = bank("fbank")

        tokens_loaded = [sem(f"tokens_loaded{c}") for c in range(5)]
        weights_loaded = [sem(f"weights_loaded{c}") for c in range(5)]
        shared_up_loaded = sem("shared_up_loaded")
        up_loaded = [sem("up_loaded1"), sem("up_loaded2")]
        up_hi_ready = sem("up_hi_ready")
        up_lo_ready = sem("up_lo_ready")
        down_loaded = sem("down_loaded")
        shared_down_loaded = sem("down_loaded0")
        ident_ready = sem("ident_ready")
        v_ones_set = sem("v_ones_set")
        q_blocks_zeroed = sem("q_blocks_zeroed")
        wqk_lo_zeroed = sem("wqk_lo_zeroed")
        zeros_set = sem("zeros_set")
        slots_zeroed = sem("slots_zeroed")
        wrouter_split = sem("wrouter_split")
        bias_spread = sem("bias_spread")
        bias_in_bank = sem("bias_in_bank")
        bias_ready = sem("bias_ready")
        variances_ready = sem("variances_ready")
        roots_ready = sem("roots_ready")
        rstd_ready = sem("rstd_ready")
        tokens_ready = sem("tokens_ready")
        pooled_ready = sem("pooled_ready")
        chunk_turned = sem("chunk_turned")
        xT_hi_ready = sem("xT_hi_ready")
        xT_lo_ready = sem("xT_lo_ready")
        logits_ready = sem("logits_ready")
        exp_logits_ready = sem("exp_logits_ready")
        dve_link = sem("dve_link")
        selectors_ready = sem("selectors_ready")
        chosen_ready = sem("chosen_ready")
        counted = sem("counted")
        counts_read = sem("counts_read")
        tile_expert_ready = sem("tile_expert_ready")
        places_ready = sem("places_ready")
        scattered = [sem("scattered0"), sem("scattered1")]
        pair_loaded = [sem(f"pair_loaded{c}") for c in range(4)]
        pair_turned = sem("pair_turned")
        pair_hi_ready = sem("pair_hi_ready")
        pair_lo_ready = sem("pair_lo_ready")
        tile_up_done = sem("tile_up_done")
        tile_relu_ready = sem("tile_relu_ready")
        tile_hidden_turned = sem("tile_hidden_turned")
        tile_squared = sem("tile_squared")
        pair_down_done = sem("pair_down_done")
        result_ready = sem("result_ready")
        result_stored = [sem("result_stored0"), sem("result_stored1")]
        rows_gathered = [sem("rows_gathered0"), sem("rows_gathered1")]
        batch_final = sem("batch_final")
        first_expert_added = sem("first_expert_added")
        xb_ready = sem("xb_ready")
        resid_loaded = [sem("s_xr0"), sem("s_xr1")]
        resid_biased = sem("resid_biased")
        scores_T_done = sem("scores_T_done")
        scores_done = sem("scores_done")
        values_done = sem("values_done")
        out_turned = sem("out_turned")
        attn_turned = sem("attn_turned")
        projected = sem("projected")
        maxes_turned = sem("maxes_turned")
        qk01_projected = sem("qk01_projected")
        qk23_projected = sem("qk23_projected")
        v_projected = sem("v_projected")
        exps_ready = sem("exps_ready")
        part01_ready = sem("part01_ready")
        part23_ready = sem("part23_ready")
        max_rows_ready = sem("max_rows_ready")
        out_kept = sem("out_kept")
        attn_T_ready = sem("attn_T_ready")
        relu_ready = sem("relu_ready")
        maxes_ready = sem("maxes_ready")
        qk01_ready = sem("qk01_ready")
        qk23_ready = sem("qk23_ready")
        v_ready = sem("v_ready")
        recips_ready = sem("recips_ready")
        attn_ready = sem("attn_ready")
        up_done = sem("up_done")
        hidden_ready = sem("hidden_ready")
        down_done = sem("down_done")
        shared_added = sem("shared_added")
        batch_added = sem("batch_added")
        spread01_done = sem("spread01_done")
        spread23_done = sem("spread23_done")
        maxes01_placed = sem("maxes01_placed")
        maxes23_placed = sem("maxes23_placed")
        stored = sem("stored")

        def wait(eng, s, n):
            if not (isinstance(n, int) and n <= 0):
                eng.wait_ge(s, n)

        def batches(body, eng, after=None, routed=None):
            for b in (-2, -1, 0, 1, 2):
                body(b, b % 2, F=b >= 1, A=b >= 0, N=b >= -1, Q=True, S=False)
                if after:
                    after(b)
            with eng.Fori(1, 3) as i:
                body(i * 2 + 1, 1, F=True, A=True, N=True, Q=True, S=False)
                body(i * 2 + 2, 0, F=True, A=True, N=True, Q=True, S=False)
            if routed:
                routed()
            with eng.Fori(3, 6) as i:
                body(i * 2 + 1, 1, F=True, A=True, N=True, Q=True, S=True)
                body(i * 2 + 2, 0, F=True, A=True, N=True, Q=True, S=True)
            for b in (13, 14, 15, 16):
                body(b, b % 2, F=True, A=b <= 15, N=b <= 14, Q=b <= 13, S=True)

        def steps(step, eng):
            for p in (-1, 0, 1, 2):
                step(p, 0, p)
            with eng.Fori(0, (PAIRS - 4) // 4) as i:
                for c in range(3, 7):
                    step(i * 4 + c, i, c)
            for p in range(PAIRS - 1, PAIRS + 1):
                step(p, 0, p)

        def has(p):
            return not isinstance(p, int) or 0 <= p < PAIRS

        def at(b, n):
            return isinstance(b, int) and b == n

        def chunk_at(b, j):
            return PREPARE.get((b, j)) if isinstance(b, int) else None

        def finals(b):
            first = (b - (ROUTED_AT + 1)) * 2
            return FINAL[b] if isinstance(b, int) else ((first, 4), (first + 1, 6))

        block = ctx.enter_context(nc.Block())

        @block.sync
        def _(sp):
            xv = x.rearrange("b (t p) d -> p (b t) d", p=P)
            ov = out.rearrange("b (t p) d -> p (b t) d", p=P)

            def tokens(k, t0, t1):
                sp.dma_start(X[:, t0:t1, :], xv[:, t0:t1, :]).then_inc(tokens_loaded[k], 16)

            tokens(0, 0, 4)
            tokens(1, 4, 8)
            for k, (dst, src) in enumerate(((wst[:], wqkvT), (rows[0:1, 0:384], bqkv), (rows[0:1, 384:512], bproj),
                                            (wrouter[:], w_router))):
                sp.dma_start(dst, src).then_inc(weights_loaded[k], 16)
            tokens(2, 8, 16)
            sp.dma_start(rawsh, w_sup).then_inc(shared_up_loaded, 16)
            tokens(3, 16, 24)
            tokens(4, 24, 32)
            sp.dma_start(wproj[:], wprojT).then_inc(weights_loaded[4], 16)
            sp.dma_start(down_w[:, 0], w_sdown.rearrange("(c p) d -> p c d", p=P)).then_inc(shared_down_loaded, 16)
            sp.wait_ge(q_blocks_zeroed, 1)

            def residual(b, r):
                sp.dma_start(resid[:, r, :].rearrange("p (t d) -> p t d", t=TT),
                             xv[:, bass.ds(b * TT, TT), :]).then_inc(resid_loaded[r], 16)

            def spread(n, r, done):
                for q in range(LANES):
                    sp.dma_start(q_blocks[32 * q:32 * q + 32, r, 2 * n:2 * n + 2, q, :].bitcast(F32),
                                 q_dense[32 * q:32 * q + 32, 2 * n:2 * n + 2, :].bitcast(F32)).then_inc(done, 16)

            def maxima(n, r, done):
                for q in range(LANES):
                    sp.dma_start(q_blocks[32 * q:32 * q + 1, r, 2 * n:2 * n + 2, q, :].bitcast(F32),
                                 max_rows[2 * q:2 * q + 2, n, :].bitcast(F32)).then_inc(done, 16)

            def body(b, r, F, A, N, Q, S):
                if A:
                    sp.wait_ge(max_rows_ready, 2 * b + 2)
                    maxima(1, r, maxes23_placed)
                if N:
                    sp.wait_ge(qk23_ready, 2 * (b + 1) + 1)
                    spread(1, 1 - r, spread23_done)
                    sp.wait_ge(max_rows_ready, 2 * (b + 1) + 1)
                    maxima(0, 1 - r, maxes01_placed)
                if Q:
                    sp.wait_ge(qk01_ready, 2 * (b + 2) + 1)
                    spread(0, r, spread01_done)
                if N:
                    if F:
                        sp.wait_ge(batch_added, b)
                    residual(b + 1, 1 - r)
                if S:
                    for c, _ in finals(b):
                        store(c)

            def store(c):
                sp.wait_ge(batch_final, c + 1)
                sp.dma_start(ov[:, bass.ds(c * TT, TT), :], X[:, bass.ds(c * TT, TT), :]).then_inc(stored, 16)

            def routed():
                sp.wait_ge(scattered[0], 16 * TILES)
                sp.wait_ge(scattered[1], 16 * TILES)

                def load(q, slot):
                    rows_ = slots[bass.ds(q * 2 * P, 2 * P), :].rearrange("(k p) d -> p k d", p=P)
                    sp.dma_start(xs[slot], rows_).then_inc(pair_loaded[slot], 16)

                def load_next(q, slot):
                    sp.wait_ge(pair_turned, q + 1)
                    load(q + 4, slot)

                def store_result(q, r):
                    sp.wait_ge(result_ready, q + 1)
                    rows_ = results[bass.ds(q * 2 * P, 2 * P), :].rearrange("(k p) d -> p k d", p=P)
                    sp.dma_start(rows_, ys[:, 2 * r:2 * r + 2, :]).then_inc(result_stored[r], 16)

                for q in range(4):
                    if q == 0:
                        sp.wait_ge(hidden_ready, (ROUTED_AT + 2) * NC)
                    if q == 2:
                        sp.wait_ge(down_done, ROUTED_AT + 2)
                    load(q, q)
                for q in range(2):
                    load_next(q, q)
                with sp.Fori(0, (PAIRS - 8) // 4) as i:
                    for c in range(2, 6):
                        load_next(i * 4 + c, c % 4)
                        store_result(i * 4 + (c - 2), c % 2)
                for q in range(PAIRS - 6, PAIRS - 4):
                    load_next(q, q % 4)
                    store_result(q - 2, q % 2)
                for q in range(PAIRS - 6, PAIRS):
                    store_result(q, q % 2)

            def after(b):
                if b == 1:
                    sp.wait_ge(tile_expert_ready, 2)
                    for e in range(LATE - 1, E):
                        sp.dma_start(down_w[:, e + 1], w_down[e].rearrange("(c p) d -> p c d", p=P)).then_inc(down_loaded, 16)

            batches(body, sp, after=after, routed=routed)
            sp.wait_ge(stored, 16 * B)

        @block.gpsimd
        def _(pool):
            nc.gpsimd.memset(ident[:], 0.0).then_inc(ident_ready, 1)
            pool.wait_ge(ident_ready, 1)
            nc.gpsimd.affine_select(out=ident[:], in_=ident[:], compare_op=ALU.not_equal, fill=1.0, base=0,
                                    pattern=[[-1, P]], channel_multiplier=1).then_inc(ident_ready, 1)
            nc.gpsimd.memset(wqk_lo[:].bitcast(F32), 0.0).then_inc(wqk_lo_zeroed, 1)
            nc.gpsimd.memset(q_blocks[:].bitcast(F32), 0.0).then_inc(q_blocks_zeroed, 1)
            nc.gpsimd.memset(zeros[:], 0.0).then_inc(zeros_set, 1)
            nc.gpsimd.memset(v_ones[:], 0.0).then_inc(v_ones_set, 1)
            pool.wait_ge(v_ones_set, 1)
            for r in range(2):
                for t in range(TT):
                    nc.gpsimd.memset(v_ones[:, r, t, 0:NH * VW].rearrange("p (h c) -> p h c", c=VW)[:, :, HD:VW],
                                     1.0).then_inc(v_ones_set, 1)

            def selectors():
                nc.gpsimd.memset(sel, 1.0).then_inc(selectors_ready, 1)
                pool.wait_ge(selectors_ready, 1)
                nc.gpsimd.affine_select(out=sel[:, 0, :], in_=sel[:, 0, :], compare_op=ALU.is_gt, fill=0.0, base=0,
                                        pattern=[[1, P]], channel_multiplier=-1).then_inc(selectors_ready, 1)
                nc.gpsimd.iota(tile_starts[:], pattern=[[P, TILES]], base=0, channel_multiplier=0,
                               allow_small_or_imprecise_dtypes=True).then_inc(selectors_ready, 1)
                nc.gpsimd.iota(tile_index[:], pattern=[[1, NT]], base=0, channel_multiplier=0,
                               allow_small_or_imprecise_dtypes=True).then_inc(selectors_ready, 1)

            def fetch(b, r):
                nc.gpsimd.tensor_copy(xb_hi[:, r, :], xT_hi[:, b * T:b * T + T].bitcast(F32)).then_inc(xb_ready, 1)
                nc.gpsimd.tensor_copy(xb_lo[:, r, :], xT_lo[:, b * T:b * T + T].bitcast(F32)).then_inc(xb_ready, 1)

            def add_bias(b, r):
                pool.wait_ge(resid_loaded[r], 16 * (b // 2 + 1))
                x2 = resid[:, r, :].rearrange("p (t d) -> p t d", t=TT)
                nc.gpsimd.tensor_tensor(x2, x2, bias_rows[:, D:].unsqueeze(1).to_broadcast([P, TT, D]),
                                        ALU.add).then_inc(resid_biased, 1)

            def dispatch(tiles):
                for t in tiles:
                    r, n = t // TT % 2, t // TT // 2
                    if t % TT == 0 and n:
                        pool.wait_ge(scattered[r], 64 * n)
                    for k in range(2):
                        pool.indirect_dma_start(
                            out=slots, out_offset=bass.IndirectOffsetOnAxis(ap=place_of[:, k, t:t + 1], axis=0),
                            in_=X[:, t, :], in_offset=None).then_inc(scattered[r], 16)

            def collect(c):
                if c >= 2:
                    pool.wait_ge(batch_final, c - 1)
                for k in range(2):
                    for t in range(TT):
                        pool.indirect_dma_start(
                            out=gathered[:, c % 2, k * TT + t, :], out_offset=None, in_=results,
                            in_offset=bass.IndirectOffsetOnAxis(ap=place_of[:, k, c * TT + t:c * TT + t + 1], axis=0),
                        ).then_inc(rows_gathered[c % 2], 16)

            def split_upper(experts):
                for e in experts:
                    k = (e - 1) % 2
                    pool.wait_ge(up_loaded[k], 16 * ((e + 1) // 2))
                    nc.gpsimd.tensor_copy(up_hi[:, e, :], raw[k][:]).then_inc(up_hi_ready, 1)
                    pool.wait_ge(up_hi_ready, e + 1)
                    nc.gpsimd.tensor_tensor(up_lo[:, e, :], raw[k][:], up_hi[:, e, :].bitcast(F32),
                                            ALU.subtract).then_inc(up_lo_ready, 1)
                    if e + 2 < FFNS:
                        pool.wait_ge(up_lo_ready, e + 1)
                        load_upper(e + 2)

            def load_upper(e):
                k = (e - 1) % 2
                pool.dma_start(raw[k][:], w_up[e - 1]).then_inc(up_loaded[k], 16)

            pool.wait_ge(xT_lo_ready, 1)
            fetch(0, 0)
            fetch(1, 1)
            selectors()
            pool.wait_ge(rstd_ready, 2)
            for c in range(CHUNKS - POOLED, CHUNKS):
                for t in range(CHUNK * c, CHUNK * c + CHUNK):
                    ins = nc.gpsimd.tensor_scalar(X[:, t, :], X[:, t, :], mean_var[:, t, 0:1], norms[:, 1, t:t + 1],
                                                  ALU.subtract, ALU.mult)
                ins.then_inc(pooled_ready, 1)
            pool.wait_ge(up_lo_ready, 1)
            load_upper(1)
            load_upper(2)
            pool.wait_ge(bias_ready, 1)
            shares = {1: range(0, 2), 2: range(2, 10), 3: range(10, 18), 4: range(18, 26), 5: range(26, 32)}
            for b in range(B):
                add_bias(b, b % 2)
                if b + 2 < B:
                    pool.wait_ge(up_done, (b + 1) * NC)
                    if b < CHUNKS * 2 - 2 and b % 2 == 0:
                        pool.wait_ge(xT_lo_ready, b // 2 + 2)
                    fetch(b + 2, b % 2)
                if b == 0:
                    split_upper(range(1, 5))
                if b in shares:
                    if b == 1:
                        pool.wait_ge(places_ready, 2)
                        pool.wait_ge(slots_zeroed, 32)
                    dispatch(shares[b])
                if b == 5:
                    split_upper(range(5, 6))
                if b == ROUTED_AT:
                    split_upper(range(6, 9))
                if b == ROUTED_AT + 1:
                    pool.wait_ge(result_stored[0], 8 * PAIRS)
                    pool.wait_ge(result_stored[1], 8 * PAIRS)
                if ROUTED_AT < b < 13:
                    collect(2 * b - 2 * (ROUTED_AT + 1))
                    collect(2 * b - 2 * (ROUTED_AT + 1) + 1)
                if b >= 13:
                    collect(b - 1)
            collect(B - 1)

        @block.scalar
        def _(act):
            def high_part(c):
                act.wait_ge(chunk_turned, c + 1)
                nc.scalar.activation(xT_hi[:, 512 * c:512 * c + 512], tbank[c % 2][:], ACT.Copy).then_inc(xT_hi_ready, 1)

            def roots(k, t0, t1):
                act.wait_ge(variances_ready, k)
                nc.scalar.activation(norms[:, 1, t0:t1], norms[:, 0, t0:t1], ACT.Sqrt).then_inc(roots_ready, 1)

            roots(1, 0, 2 * CHUNK)
            high_part(0)
            roots(2, 2 * CHUNK, TILES)
            act.wait_ge(bias_ready, 1)
            act.wait_ge(shared_up_loaded, 16)
            nc.scalar.activation(up_hi[:, 0, :], rawsh, ACT.Copy).then_inc(up_hi_ready, 1)

            def after(b):
                if b == -2:
                    act.wait_ge(zeros_set, 1)
                    half = NT * P // 2
                    for k in range(2):
                        act.dma_start(slots[k * half:k * half + half].rearrange("(p t) d -> p t d", p=P),
                                      zeros[:].unsqueeze(1).to_broadcast([P, NT // 2, D])).then_inc(slots_zeroed, 16)
                    for e in range(LATE - 1):
                        act.dma_start(down_w[:, e + 1], w_down[e].rearrange("(c p) d -> p c d", p=P)).then_inc(down_loaded, 16)
                if b == -1:
                    act.wait_ge(logits_ready, CHUNKS)
                    nc.scalar.activation(table(0).rearrange("p t e -> p (t e)"), obank[:, 0:TILES * E], ACT.Exp,
                                         scale=-1.0).then_inc(exp_logits_ready, 1)

            def ffn(b, k):
                if k in FILL and FILL[k][0] == "up":
                    n = FILL[k][1]
                    act.wait_ge(up_done, b * NC + n + 1)
                    wait(act, hidden_ready, b * NC + n)
                    nc.scalar.activation(relu_T[:], fbank[:], ACT.Relu).then_inc(relu_ready, 1)
                    act.wait_ge(relu_ready, b * NC + n + 1)
                    wait(act, down_done, b)
                    nc.scalar.activation(hidden_T[:, 2 * n:2 * n + 2, :].rearrange("p c m -> p (c m)"), relu_T[:],
                                         ACT.Square).then_inc(hidden_ready, 1)

            def partial(b, r, n, qk, produced, s_t, freed):
                act.wait_ge(produced, 2 * b + qk + 1)
                wait(act, freed[0], freed[1])
                for g in range(2):
                    ins = nc.scalar.activation(taken[:, qk, g, :], pbank[:, g * T:g * T + T], ACT.Identity,
                                               bias=bias[:, 10 + 4 * qk + 2 * n + g:11 + 4 * qk + 2 * n + g],
                                               scale=bias[:, 8 + qk:9 + qk])
                ins.then_inc(s_t, 1)

            def keep_output(b, n):
                act.wait_ge(values_done, b * 8 + 4 * n + 4)
                wait(act, out_turned, 2 * b + n - 1)
                nc.scalar.activation(out_raw[:, n], obank[:].rearrange("p (g q) -> p g q", g=2), ACT.Copy).then_inc(out_kept, 1)

            def keep_maxima(b, n, loaded):
                act.wait_ge(maxes_turned, 2 * b + n + 1)
                wait(act, loaded, 64 * b)
                nc.scalar.activation(max_rows[:, n, :], wbank[0:8, 0:T], ACT.Copy).then_inc(max_rows_ready, 1)

            def body(b, r, F, A, N, Q, S):
                for j in range(SLOTS):
                    if F and j == 1:
                        keep_output(b - 1, 1)
                    if A and j == 5:
                        keep_output(b, 0)
                    for u in (2 * j, 2 * j + 1):
                        if A:
                            act.wait_ge(scores_T_done, b * NU + u + 1)
                            wait(act, values_done, b * 8 + j - 1)
                            nc.scalar.activation(probs[:, u % 4, :], tbank[u % 2][:], ACT.Exp, scale=SCALE).then_inc(exps_ready, 1)
                    qk = j // 2 % 2
                    if N and j in (0, 2):
                        partial(b + 1, 1 - r, 1, qk, qk23_projected, part23_ready, (qk01_ready, 2 * (b + 1) + qk + 1))
                    if Q and j in (4, 6):
                        partial(b + 2, r, 0, qk, qk01_projected, part01_ready, (qk23_ready, 2 * (b + 1) + qk + 1))
                    if A and j == 0:
                        keep_maxima(b, 1, maxes23_placed)
                    if F and j == 3:
                        act.wait_ge(attn_turned, b)
                        wait(act, projected, b - 1)
                        nc.scalar.activation(attn_T[:], wbank[:, 0:T], ACT.Copy).then_inc(attn_T_ready, 1)
                    if N and j == 4:
                        keep_maxima(b + 1, 0, maxes01_placed)
                    if N:
                        ffn(b + 1, 2 * j)
                    if chunk_at(b, j):
                        high_part(chunk_at(b, j))
                    if N:
                        ffn(b + 1, 2 * j + 1)

            def step(p, i, c):
                if has(p + 1):
                    act.wait_ge(pair_turned, p + 2)
                    nc.scalar.activation(pair_hi[:].rearrange("p k d -> p (k d)"), sbank[0][:, 0:2 * P],
                                         ACT.Copy).then_inc(pair_hi_ready, 1)
                if has(p):
                    for k in range(2):
                        act.wait_ge(tile_hidden_turned, p * 2 + (k + 1))
                        nc.scalar.activation(hr[:, k].rearrange("p c m -> p (c m)"), (wbank, fbank)[k][:],
                                             ACT.Square).then_inc(tile_squared, 1)

            batches(body, act, after=after, routed=lambda: steps(step, act))

        @block.vector
        def _(dve):
            chain = [0]

            def link(ins):
                chain[0] += 1
                ins.then_inc(dve_link, 1)
                dve.wait_ge(dve_link, chain[0])

            def statistics(t0, t1):
                for t in range(t0, t1):
                    nc.vector.bn_stats(stats[:, t, :], X[:, t, :]).then_inc(dve_link, 1)
                chain[0] += t1 - t0
                dve.wait_ge(dve_link, chain[0])
                for t in range(t0, t1):
                    nc.vector.bn_aggr(mean_var[:, t, :], stats[:, t, :]).then_inc(dve_link, 1)
                chain[0] += t1 - t0
                dve.wait_ge(dve_link, chain[0])
                nc.vector.tensor_scalar(norms[:, 0, t0:t1], mean_var[:, t0:t1, 1], EPS, None, ALU.add).then_inc(variances_ready, 1)

            def inverse_roots(k, t0, t1):
                dve.wait_ge(roots_ready, k)
                v, y, z, w = (norms[:, n, t0:t1] for n in range(4))
                link(nc.vector.reciprocal(z, y))
                link(nc.vector.tensor_tensor(w, z, z, ALU.mult))
                link(nc.vector.tensor_tensor(w, w, v, ALU.mult))
                link(nc.vector.tensor_scalar(w, w, -0.5, 1.5, ALU.mult, ALU.add))
                nc.vector.tensor_tensor(y, w, z, ALU.mult).then_inc(rstd_ready, 1)
                dve.wait_ge(rstd_ready, k)

            def standardise(c):
                for t in range(CHUNK * c, CHUNK * c + CHUNK):
                    ins = nc.vector.tensor_scalar(X[:, t, :], X[:, t, :], mean_var[:, t, 0:1], norms[:, 1, t:t + 1],
                                                  ALU.subtract, ALU.mult)
                ins.then_inc(tokens_ready, 1)

            def low_part(c):
                dve.wait_ge(xT_hi_ready, c + 1)
                cols = slice(512 * c, 512 * c + 512)
                nc.vector.tensor_tensor(xT_lo[:, cols], tbank[c % 2][:], xT_hi[:, cols].bitcast(F32),
                                        ALU.subtract).then_inc(xT_lo_ready, 1)

            def prepare(c):
                if 2 <= c < CHUNKS - POOLED:
                    standardise(c)
                if c >= 2:
                    low_part(c - 1)

            nc.vector.memset(wqk_hi[:].bitcast(F32), 0.0)
            nc.vector.memset(rows[0:1, 512:2048], 0.0)
            nc.vector.memset(bias[:], 0.0)
            dve.wait_ge(tokens_loaded[0], 16)
            dve.wait_ge(tokens_loaded[1], 16)
            statistics(0, 2 * CHUNK)
            inverse_roots(1, 0, 2 * CHUNK)
            standardise(0)
            standardise(1)
            for k in range(4):
                dve.wait_ge(weights_loaded[k], 16)
            dve.wait_ge(wqk_lo_zeroed, 1)
            link(nc.vector.tensor_copy(wqkv_hi[:], wst[:]))
            nc.vector.tensor_tensor(wqkv_lo[:], wst[:], wqkv_hi[:].bitcast(F32), ALU.subtract)
            link(nc.vector.tensor_copy(wrouter_hi[:], wrouter[:]))
            nc.vector.tensor_tensor(wrouter_lo[:], wrouter[:], wrouter_hi[:].bitcast(F32), ALU.subtract).then_inc(wrouter_split, 1)
            low_part(0)
            for qk in range(2):
                for src, dst in ((wqkv_hi, wqk_hi), (wqkv_lo, wqk_lo)):
                    for p in PART:
                        o = dst[:, qk].rearrange("p g (q c) -> p (g q) c", c=32)[:, :, p:p + 8]
                        i = src[:, qk * D:(qk + 1) * D].bitcast(F32).rearrange("p (h d) -> p h d", d=HD)
                        nc.vector.tensor_copy(o, i)
                for p in PART:
                    o = rows[0:1, 512 + 512 * qk:1024 + 512 * qk].rearrange("p (h c) -> p h c", c=32)[:, :, p:p + 8]
                    nc.vector.tensor_copy(o, rows[0:1, qk * D:(qk + 1) * D].rearrange("p (h d) -> p h d", d=HD))
                p = PART[LOW[qk]]
                m = rows[0:1, 1536 + P * qk:1536 + P * qk + P].rearrange("p (q c) -> p q c", c=32)
                nc.vector.memset(m[:, :, p:p + 8], 1.0)
            nc.vector.memset(rows[0:1, 1024:1536].rearrange("p (h c) -> p h c", c=32)[:, :, 0:1], 1.0)
            nc.vector.memset(rows[0:1, 1792:1920], 1.0).then_inc(bias_spread, 1)
            for k in range(2, 5):
                dve.wait_ge(tokens_loaded[k], 16)
            statistics(2 * CHUNK, TILES)
            dve.wait_ge(bias_in_bank, 1)
            link(nc.vector.tensor_copy(bias[:, 0:10], wbank[:, 0:10]))
            for qk in range(2):
                nc.vector.tensor_scalar(bias[:, 10 + 4 * qk:14 + 4 * qk], bias[:, 4 * qk:4 * qk + 4],
                                        bias[:, 8 + qk:9 + qk], None, ALU.mult)
            nc.vector.tensor_copy(bias_rows[:], wbank[:, 128:384]).then_inc(bias_ready, 1)

            inverse_roots(2, 2 * CHUNK, TILES)
            dve.wait_ge(up_hi_ready, 1)
            nc.vector.tensor_tensor(up_lo[:, 0, :], rawsh, up_hi[:, 0, :].bitcast(F32),
                                    ALU.subtract).then_inc(up_lo_ready, 1)
            Xf = X[:].rearrange("p t d -> p (t d)")

            def bc(ap):
                return ap.unsqueeze(2).to_broadcast([P, TILES, E])

            ends = tile_counts[:, 3, :]

            def choose(j):
                p, work, rest = table(0), table(3), table(4)
                wt = rank[:].unsqueeze(1).to_broadcast([P, TILES, E])

                def best(k, src):
                    link(nc.vector.tensor_reduce(chosen_rows[:, k, :], src, AX_X, ALU.max))
                    link(nc.vector.tensor_tensor(work, src, bc(chosen_rows[:, k, :]), ALU.is_equal))
                    link(nc.vector.tensor_tensor(work, work, wt, ALU.mult))

                def first(k):
                    link(nc.vector.tensor_reduce(chosen_rows[:, 2, :], work, AX_X, ALU.max))
                    link(nc.vector.tensor_tensor(table(1 + k), work, bc(chosen_rows[:, 2, :]), ALU.is_equal))

                if j == 0:
                    for e in range(E):
                        nc.vector.memset(rank[:, e:e + 1], float(E - e))
                    dve.wait_ge(exp_logits_ready, 1)
                    link(nc.vector.tensor_scalar(p, p, 1.0, None, ALU.add))
                if j == 1:
                    link(nc.vector.reciprocal(p, p))
                if j == 2:
                    best(0, p)
                if j == 3:
                    first(0)
                if j == 4:
                    link(nc.vector.tensor_scalar(rest, table(1), -2.0, None, ALU.mult))
                    link(nc.vector.tensor_tensor(rest, rest, p, ALU.add))
                if j == 5:
                    best(1, rest)
                if j == 6:
                    first(1)
                    nc.vector.tensor_tensor(table(5), table(1), table(2), ALU.add).then_inc(chosen_ready, 1)
                if j == 7:
                    link(nc.vector.tensor_tensor(chosen_rows[:, 2, :], chosen_rows[:, 0, :], chosen_rows[:, 1, :], ALU.add))
                    link(nc.vector.tensor_scalar(chosen_rows[:, 2, :], chosen_rows[:, 2, :], 1e-6, None, ALU.add))
                    link(nc.vector.reciprocal(chosen_rows[:, 3, :], chosen_rows[:, 2, :]))
                    for k in range(2):
                        link(nc.vector.tensor_tensor(chosen_rows[:, k, :], chosen_rows[:, k, :], chosen_rows[:, 3, :], ALU.mult))

            def place(j):
                before, total, spot = table(6), table(7), table(0)
                turns = [total, table(3), table(4)]
                half = TILES * E

                def sums(k):
                    a, o = turns[0 if k == 1 else 1 + k % 2], turns[2 - k % 2]
                    step = 1 << (k - 1)
                    nc.vector.tensor_copy(o[:, 0:step], a[:, 0:step])
                    link(nc.vector.tensor_tensor(o[:, step:], a[:, step:], a[:, 0:TILES - step], ALU.add))

                levels = TILES.bit_length() - 1
                upto = turns[2 - levels % 2]
                if j == 0:
                    dve.wait_ge(counted, 1)
                    nc.vector.memset(tile_counts[:, 4, :], 0.0)
                    nc.vector.tensor_copy(before.rearrange("p t e -> p (t e)"), fbank[:, 0:half]).then_inc(counts_read, 1)
                    nc.vector.tensor_copy(total.rearrange("p t e -> p (t e)"), fbank[:, half:2 * half]).then_inc(counts_read, 1)
                    dve.wait_ge(counts_read, 2)
                if j == 1:
                    for k in range(1, 1 + levels):
                        sums(k)
                if j == 2:
                    cmp = spot.rearrange("p t e -> p (t e)").rearrange("p (e t) -> p e t", e=E)
                    link(nc.vector.tensor_tensor(cmp, upto[:, TILES - 1, :].unsqueeze(2).to_broadcast([P, E, TILES]),
                                                 tile_starts[:].unsqueeze(1).to_broadcast([P, E, TILES]), ALU.is_gt))
                    link(nc.vector.tensor_reduce(tile_counts[:, 0, :], cmp, AX_X, ALU.add))
                    for c in range(3):
                        step = 1 << c
                        nc.vector.tensor_copy(tile_counts[:, c + 1, 0:step], tile_counts[:, c, 0:step])
                        link(nc.vector.tensor_tensor(tile_counts[:, c + 1, step:], tile_counts[:, c, step:], tile_counts[:, c, 0:E - step], ALU.add))
                    link(nc.vector.tensor_scalar(tile_counts[:, 4, 1:E], ends[:, 0:E - 1], float(P), None, ALU.mult))
                if j == 3:
                    link(nc.vector.tensor_tensor(spot[:, 1:], before[:, 1:], upto[:, 0:TILES - 1], ALU.add))
                    link(nc.vector.tensor_copy(spot[:, 0:1], before[:, 0:1]))
                    link(nc.vector.tensor_tensor(spot, spot, tile_counts[:, 4, :].unsqueeze(1).to_broadcast([P, TILES, E]), ALU.add))
                if j in (3, 4):
                    k = j - 3
                    link(nc.vector.tensor_tensor(before, spot, table(1 + k), ALU.mult))
                    link(nc.vector.tensor_reduce(chosen_rows[:, 2, :], before, AX_X, ALU.add))
                    nc.vector.tensor_copy(place_of[:, k, :], chosen_rows[:, 2, :]).then_inc(places_ready, 1)
                    dve.wait_ge(places_ready, k + 1)
                if j == 7:
                    nc.vector.memset(tile_expert[:], 0.0).then_inc(tile_expert_ready, 1)
                    dve.wait_ge(tile_expert_ready, 1)
                    for e in range(E - 1):
                        link(nc.vector.scalar_tensor_tensor(out=tile_expert[:], in0=tile_index[:], scalar=ends[0:1, e:e + 1],
                                                            in1=tile_expert[:], op0=ALU.is_ge, op1=ALU.add))
                    nc.vector.tensor_scalar(tile_weights[:], tile_expert[:], 1.0, float(H), ALU.add, ALU.mult).then_inc(tile_expert_ready, 1)

            def ffn(b, k, q):
                if k not in FILL:
                    return
                if FILL[k][0] == "down":
                    dve.wait_ge(down_done, b + 1)
                    dve.wait_ge(resid_biased, b + 1)
                    y = resid[:, q, :]
                    nc.vector.tensor_tensor(y, fbank[:, 0:T], y, ALU.add).then_inc(shared_added, 1)

            def split(b, r, n, qk, s_t, done):
                dve.wait_ge(s_t, 2 * b + qk + 1)
                if qk == 0:
                    wait(dve, (spread01_done, spread23_done)[n], 64 * b)
                for g in range(2):
                    dst = q_dense[:, 2 * n + g, :] if qk == 0 else k_parts[:, r, 2 * n + g, :]
                    ins = nc.vector.scalar_tensor_tensor(
                        out=dst, in0=pbank[:, g * T:g * T + T], scalar=bias[:, 4 * qk + 2 * n + g:4 * qk + 2 * n + g + 1],
                        in1=taken[:, qk, g, :].bitcast(F32), op0=ALU.add, op1=ALU.subtract)
                ins.then_inc(done, 1)

            def normalise(b, n):
                dve.wait_ge(out_turned, 2 * b + n + 1)
                wait(dve, attn_turned, b)
                m = wbank[:].rearrange("p (q h c) -> p q h c", q=TT, c=32)
                nc.vector.reciprocal(recips[:, n, :].rearrange("p (q h c) -> p q h c", q=TT, c=1), m[:, :, :, 8:9]).then_inc(recips_ready, 1)
                dve.wait_ge(recips_ready, 2 * b + n + 1)
                nc.vector.tensor_tensor(
                    attn[:, :, 64 * n:64 * n + 64].rearrange("p q (h d) -> p q h d", d=HD), m[:, :, :, 0:8],
                    recips[:, n, :].rearrange("p (q h) -> p q h", q=TT).unsqueeze(3).to_broadcast([P, TT, 8, HD]),
                    ALU.mult).then_inc(attn_ready, 1)

            def body(b, r, F, A, N, Q, S):
                for j in range(SLOTS):
                    if chunk_at(b, j):
                        prepare(chunk_at(b, j))
                    if at(b, 0):
                        choose(j)
                    if at(b, 1):
                        place(j)
                    if N and j == 4:
                        dve.wait_ge(v_projected, b + 2)
                        nc.vector.tensor_tensor(
                            v_ones[:, 1 - r, :, 0:NH * VW].rearrange("p t (h c) -> p t h c", c=VW)[:, :, :, 0:HD],
                            pbank[:, 0:2 * D].rearrange("p (t h d) -> p t h d", t=TT, d=HD),
                            bias_rows[:, 0:D].rearrange("p (h d) -> p h d", d=HD).unsqueeze(1).to_broadcast([P, TT, NH, HD]),
                            ALU.add).then_inc(v_ready, 1)
                    for h in (2 * j, 2 * j + 1):
                        if N:
                            dve.wait_ge(scores_done, (b + 1) * NU + h + 1)
                            wait(dve, maxes_turned, 2 * b + 1 + h // 8)
                            nc.vector.tensor_reduce(maxes[:, h // 8, :, h % 4, (h // 4) % 2],
                                                    sbank[h % 2][:].rearrange("p (q k) -> p q k", q=TT), AX_X, ALU.max,
                                                    negate=True).then_inc(maxes_ready, 1)
                        if h == 2 * j and N and j in (1, 3):
                            split(b + 1, 1 - r, 1, j // 2, part23_ready, qk23_ready)
                        if h == 2 * j and Q and j in (5, 7):
                            split(b + 2, r, 0, j // 2 - 2, part01_ready, qk01_ready)
                    if N:
                        ffn(b + 1, 2 * j, 1 - r)
                    if F and j == 2:
                        normalise(b - 1, 1)
                    if F and j == 5:
                        dve.wait_ge(projected, b)
                        dve.wait_ge(shared_added, b)
                        dve.wait_ge(scattered[1 - r], (b - 1 - (1 - r)) * 32 + 64)
                        nc.vector.tensor_tensor(Xf[:, bass.ds((b - 1) * TT * D, TT * D)], wbank[:, 0:T],
                                                resid[:, 1 - r, :], ALU.add).then_inc(batch_added, 1)
                    if A and j == 6:
                        normalise(b, 0)
                    if S:
                        for c, place_ in finals(b):
                            if place_ == j:
                                finish(c, c % 2 if isinstance(c, int) else j // 2 - 2)
                    if N:
                        ffn(b + 1, 2 * j + 1, 1 - r)

            def finish(c, q):
                dve.wait_ge(batch_added, c + 1)
                dve.wait_ge(rows_gathered[q], (c // 2 + 1) * 64 if isinstance(c, int) else (c - (0, 1)[q]) * 32 + 64)
                for k in range(2):
                    for t in range(TT):
                        o = Xf[:, bass.ds((c * TT + t) * D, D)]
                        w = chosen_rows[:, k, bass.ds(c * TT + t, 1)]
                        ins = nc.vector.scalar_tensor_tensor(out=o, in0=gathered[:, q, k * TT + t, :], scalar=w, in1=o,
                                                             op0=ALU.mult, op1=ALU.add)
                        if k == 0:
                            ins.then_inc(first_expert_added, 1)
                    if k == 0:
                        dve.wait_ge(first_expert_added, (c + 1) * TT)
                ins.then_inc(batch_final, 1)

            def after(b):
                if b == -1:
                    low_part(CHUNKS - 1)

            def step(p, i, c):
                if has(p):
                    for k in range(2):
                        dve.wait_ge(tile_up_done, p * 2 + (k + 1))
                        nc.vector.tensor_scalar(rr[:, k, :], tbank[k][:], 0.0, None, ALU.max).then_inc(tile_relu_ready, 1)
                if has(p + 1):
                    dve.wait_ge(pair_hi_ready, p + 2)
                    nc.vector.tensor_tensor(pair_lo[:].rearrange("p k d -> p (k d)"), sbank[0][:, 0:2 * P],
                                            pair_hi[:].bitcast(F32).rearrange("p k d -> p (k d)"),
                                            ALU.subtract).then_inc(pair_lo_ready, 1)
                if has(p - 1):
                    r = (c - 1) % 2
                    dve.wait_ge(pair_down_done, p)
                    wait(dve, result_stored[r], i * 32 + (c - 1) // 2 * 16)
                    nc.vector.tensor_copy(ys[:, 2 * r:2 * r + 2, :].rearrange("p k d -> p (k d)"),
                                          pbank[:, 0:2 * D]).then_inc(result_ready, 1)

            batches(body, dve, after=after, routed=lambda: steps(step, dve))

        @block.tensor
        def _(pe):
            def three(o, lh, ll, rh, rl):
                nc.tensor.matmul(o, lh, rl, start=True, stop=False)
                nc.tensor.matmul(o, ll, rh, start=False, stop=False)
                return nc.tensor.matmul(o, lh, rh, start=False, stop=True)

            def transposed(c):
                if c < CHUNKS - POOLED:
                    pe.wait_ge(tokens_ready, c + 1)
                else:
                    pe.wait_ge(pooled_ready, c + 1 - (CHUNKS - POOLED))
                wait(pe, xT_lo_ready, c - 1)
                for t in range(CHUNK):
                    ins = nc.tensor.transpose(tbank[c % 2][:, t * P:t * P + P], X[:, CHUNK * c + t, :], ident[:])
                ins.then_inc(chunk_turned, 1)

            def route(c):
                pe.wait_ge(xT_lo_ready, c + 1)
                for t in range(CHUNK * c, CHUNK * c + CHUNK):
                    cols = slice(t * P, t * P + P)
                    ins = three(obank[:, t * E:t * E + E], xT_hi[:, cols], xT_lo[:, cols], wrouter_hi[:], wrouter_lo[:])
                ins.then_inc(logits_ready, 1)

            pe.wait_ge(ident_ready, 2)
            transposed(0)
            pe.wait_ge(bias_spread, 1)
            one = rows[0:1, 1792:1793]
            for qk in range(2):
                for g in range(GROUPS):
                    a = 512 + 512 * qk + P * g
                    nc.tensor.matmul(wbank[:, 4 * qk + g:4 * qk + g + 1], rows[0:1, a:a + P], one, start=True, stop=True)
                a = 1536 + P * qk
                nc.tensor.matmul(wbank[:, 8 + qk:9 + qk], rows[0:1, a:a + P], one, start=True, stop=True)
            nc.tensor.matmul(wbank[:, 128:384], rows[0:1, 1792:1920], rows[0:1, 256:512],
                             start=True, stop=True).then_inc(bias_in_bank, 1)
            pe.wait_ge(wrouter_split, 1)

            def count():
                pe.wait_ge(chosen_ready, 1)
                pe.wait_ge(selectors_ready, 4)
                pe.wait_ge(shared_added, 2)
                for k in range(2):
                    ins = nc.tensor.matmul(fbank[:, k * TILES * E:(k + 1) * TILES * E], sel[:, k, :],
                                           table(5).rearrange("p t e -> p (t e)"), start=True, stop=True)
                ins.then_inc(counted, 1)

            def ffn(b, k, q):
                if k not in FILL:
                    return
                kind, n = FILL[k]
                if kind == "up":
                    wait(pe, relu_ready, b * NC + n)
                    if n == 0:
                        wait(pe, shared_added, b)
                        if isinstance(b, int) and b == 2:
                            pe.wait_ge(counts_read, 2)
                    for c in range(2):
                        w = slice((2 * n + c) * P, (2 * n + c + 1) * P)
                        ins = three(fbank[:, c * T:c * T + T], up_hi[:, 0, w], up_lo[:, 0, w], xb_hi[:, q, :], xb_lo[:, q, :])
                    ins.then_inc(up_done, 1)
                else:
                    pe.wait_ge(hidden_ready, b * NC + 2)
                    for t in range(TT):
                        for c in range(HC):
                            ins = nc.tensor.matmul(fbank[:, t * D:t * D + D], hidden_T[:, c, t * P:t * P + P],
                                                   down_w[:, 0, c, :], start=c == 0, stop=c == HC - 1)
                    ins.then_inc(down_done, 1)

            def project(b, r, n, qk, done):
                wait(pe, xb_ready, 2 * (b + 1))
                for g in range(2):
                    w = 2 * n + g
                    ins = three(pbank[:, g * T:g * T + T], wqk_hi[:, qk, w, :], wqk_lo[:, qk, w, :], xb_hi[:, r, :], xb_lo[:, r, :])
                ins.then_inc(done, 1)

            def turn(b, n):
                pe.wait_ge(out_kept, 2 * b + n + 1)
                for t in range(TT):
                    for g in range(2):
                        ins = nc.tensor.transpose(wbank[:, (2 * t + g) * P:(2 * t + g) * P + P],
                                                  out_raw[:, n, g, t * P:t * P + P], ident[:])
                ins.then_inc(out_turned, 1)

            def turn_max(b, n):
                pe.wait_ge(maxes_ready, b * NU + 8 * n + 8)
                for t in range(TT):
                    ins = nc.tensor.transpose(wbank[0:8, t * P:t * P + P],
                                              maxes[:, n, t].rearrange("p q g -> p (q g)"), ident[:])
                ins.then_inc(maxes_turned, 1)

            def values(b, j, r):
                g, kt = j // 2, j % 2
                pe.wait_ge(exps_ready, b * NU + 2 * j + 2)
                if j == 0:
                    pe.wait_ge(v_ready, b + 1)
                    wait(pe, out_kept, 2 * b)
                if j == 4:
                    pe.wait_ge(out_kept, 2 * b + 1)
                for q in range(LANES):
                    ins = nc.tensor.matmul(obank[32 * q:32 * q + 32, (g % 2) * T:(g % 2) * T + T],
                                           v_ones[:, r, kt, (4 * g + q) * VW:(4 * g + q) * VW + 32],
                                           probs[:, (2 * j + q // 2) % 4, (q % 2) * T:(q % 2) * T + T],
                                           start=kt == 0, stop=kt == 1)
                ins.then_inc(values_done, 1)

            def body(b, r, F, A, N, Q, S):
                for j in range(SLOTS):
                    if at(b, -1) and j == 0:
                        pe.wait_ge(q_blocks_zeroed, 1)
                        pe.wait_ge(v_ones_set, 5)
                        pe.wait_ge(weights_loaded[4], 16)
                        pe.wait_ge(up_lo_ready, 1)
                        pe.wait_ge(shared_down_loaded, 16)
                    if at(b, 0) and j == 1:
                        pe.wait_ge(exp_logits_ready, 1)
                    if A:
                        if j == 0:
                            pe.wait_ge(maxes01_placed, 64 * (b + 1))
                        if j == 4:
                            pe.wait_ge(maxes23_placed, 64 * (b + 1))
                        for u in (2 * j, 2 * j + 1):
                            g, kt, half = u // 4, (u // 2) % 2, u % 2
                            wait(pe, exps_ready, b * NU + u - 1)
                            nc.tensor.matmul(tbank[u % 2][:], k_parts[:, r, g, kt * P:kt * P + P],
                                             q_blocks[:, r, g, 2 * half:2 * half + 2, :], start=True, stop=True).then_inc(scores_T_done, 1)
                    if N and j == 4:
                        pe.wait_ge(qk23_ready, 2 * (b + 1) + 2)
                        for t in range(TT):
                            ins = three(pbank[:, t * D:t * D + D], xb_hi[:, 1 - r, t * P:t * P + P],
                                        xb_lo[:, 1 - r, t * P:t * P + P], wqkv_hi[:, 2 * D:], wqkv_lo[:, 2 * D:])
                        ins.then_inc(v_projected, 1)
                    for h in (2 * j, 2 * j + 1):
                        if N:
                            g, q = h // 4, h % 4
                            if h == 0:
                                pe.wait_ge(qk01_ready, 2 * (b + 1) + 2)
                                pe.wait_ge(spread01_done, 64 * (b + 2))
                            if h == 8:
                                pe.wait_ge(qk23_ready, 2 * (b + 1) + 2)
                                pe.wait_ge(spread23_done, 64 * (b + 2))
                            wait(pe, maxes_ready, (b + 1) * NU + h - 1)
                            for t in range(TT):
                                ins = nc.tensor.matmul(sbank[h % 2][:, t * T:t * T + T],
                                                       q_blocks[:, 1 - r, g, q, t * P:t * P + P], k_parts[:, 1 - r, g, :],
                                                       start=True, stop=True)
                            ins.then_inc(scores_done, 1)
                        if N and h % 2 == 0:
                            ffn(b + 1, h, 1 - r)
                    if N and j == 0:
                        wait(pe, qk01_ready, 2 * (b + 1) + 2)
                        project(b + 1, 1 - r, 1, 0, qk23_projected)
                    if N and j == 2:
                        pe.wait_ge(qk23_ready, 2 * (b + 1) + 1)
                        project(b + 1, 1 - r, 1, 1, qk23_projected)
                    if Q and j == 4:
                        if N:
                            pe.wait_ge(v_ready, b + 2)
                        project(b + 2, r, 0, 0, qk01_projected)
                    if Q and j == 6:
                        pe.wait_ge(qk01_ready, 2 * (b + 2) + 1)
                        project(b + 2, r, 0, 1, qk01_projected)
                    if A and j == 0:
                        pe.wait_ge(max_rows_ready, 2 * b + 1)
                        wait(pe, attn_ready, 2 * b - 1)
                        turn_max(b, 1)
                    if F and j == 2:
                        if A:
                            pe.wait_ge(max_rows_ready, 2 * b + 2)
                        else:
                            pe.wait_ge(attn_ready, 2 * b - 1)
                        turn(b - 1, 1)
                    if F and j == 3:
                        pe.wait_ge(attn_ready, 2 * b)
                        for t in range(TT):
                            ins = nc.tensor.transpose(wbank[:, t * P:t * P + P], attn[:, t, :], ident[:])
                        ins.then_inc(attn_turned, 1)
                    if N and j == 4:
                        if F:
                            pe.wait_ge(attn_T_ready, b)
                        elif A:
                            pe.wait_ge(max_rows_ready, 2 * b + 2)
                        turn_max(b + 1, 0)
                    if F and j == 5:
                        pe.wait_ge(attn_T_ready, b)
                        if N:
                            pe.wait_ge(max_rows_ready, 2 * b + 3)
                        for t in range(TT):
                            ins = nc.tensor.matmul(wbank[:, t * D:t * D + D], attn_T[:, t * P:t * P + P], wproj[:],
                                                   start=True, stop=True)
                        ins.then_inc(projected, 1)
                    if A and j == 6:
                        if F:
                            pe.wait_ge(batch_added, b)
                        elif N:
                            pe.wait_ge(max_rows_ready, 2 * b + 3)
                        turn(b, 0)
                    if chunk_at(b, j):
                        transposed(chunk_at(b, j))
                        route(chunk_at(b, j) - 1)
                    if j == 0 and F:
                        values(b - 1, 7, 1 - r)
                    if j and A:
                        values(b, j - 1, r)
                    if N:
                        ffn(b + 1, 2 * j + 1, 1 - r)

            experts = [[pe.alloc_register(f"expert{r}{k}") for k in range(2)] for r in range(2)]

            Uhf, Ulf = (w[:].rearrange("p e h -> p (e h)") for w in (up_hi, up_lo))
            Dnf = down_w[:].rearrange("p e c d -> p (e c d)")

            def step(p, i, c):
                now, last = experts[c % 2], experts[(c - 1) % 2]

                def start(reg):
                    return pe.snap(reg, min_val=H, max_val=E * H)

                if has(p):
                    pe.wait_ge(pair_lo_ready, p + 1)
                    wait(pe, tile_relu_ready, p * 2)
                    for k in range(2):
                        cols = bass.ds(start(now[k]), H)
                        three(tbank[k][:], pair_hi[:, k, :], pair_lo[:, k, :], Uhf[:, cols], Ulf[:, cols]).then_inc(tile_up_done, 1)
                if has(p + 1):
                    pe.wait_ge(pair_loaded[(c + 1) % 4], i * 16 + ((c + 1) // 4 + 1) * 16)
                    for k in range(2):
                        ins = nc.tensor.transpose(sbank[0][:, k * P:k * P + P], xs[(c + 1) % 4][:, k, :], ident[:])
                    ins.then_inc(pair_turned, 1)
                if has(p - 1):
                    wait(pe, result_ready, p - 1)
                    for k in range(2):
                        pe.wait_ge(tile_squared, p * 2 + (k - 1))
                        at = start(last[k])
                        for m in range(HC):
                            ins = nc.tensor.matmul(pbank[:, k * D:k * D + D], hr[:, k, m, :],
                                                   Dnf[:, bass.ds(at + m * D, D)], start=m == 0, stop=m == HC - 1)
                    ins.then_inc(pair_down_done, 1)
                if has(p + 1):
                    pe.reg_load(last, tile_weights[0:1, bass.ds(p * 2 + 2, 2)])
                if has(p):
                    for k in range(2):
                        pe.wait_ge(tile_relu_ready, p * 2 + (k + 1))
                        for m in range(HC):
                            ins = nc.tensor.transpose((wbank, fbank)[k][:, m * P:m * P + P],
                                                      rr[:, k, m * P:m * P + P], ident[:])
                        ins.then_inc(tile_hidden_turned, 1)

            def routed():
                pe.wait_ge(maxes_ready, (ROUTED_AT + 2) * NU)
                pe.wait_ge(exps_ready, (ROUTED_AT + 1) * NU)
                pe.wait_ge(qk01_ready, 2 * (ROUTED_AT + 2) + 2)
                pe.wait_ge(attn_ready, 2 * ROUTED_AT + 1)
                pe.wait_ge(relu_ready, (ROUTED_AT + 2) * NC)
                pe.wait_ge(shared_added, ROUTED_AT + 2)
                pe.wait_ge(tile_expert_ready, 2)
                pe.wait_ge(up_lo_ready, FFNS)
                pe.wait_ge(down_loaded, 16 * E)
                steps(step, pe)
                pe.wait_ge(result_ready, PAIRS)

            def after(b):
                if b == -1:
                    route(CHUNKS - 1)
                    pe.wait_ge(bias_ready, 1)
                if b == 0:
                    count()

            batches(body, pe, after=after, routed=routed)


def kernel(L0_attn_x, L0_attn_qkv_w, L0_attn_qkv_b, L0_attn_proj_w, L0_attn_proj_b, L0_ffn_W_router,
           L0_ffn_W_up, L0_ffn_W_down, L0_ffn_W_sh_up, L0_ffn_W_sh_down):
    import numpy as np
    import concourse.bacc as bacc
    from concourse.bass_utils import run_bass_kernel_spmd

    nc = bacc.Bacc("TRN2", target_bir_lowering=False, num_devices=1)
    given = {
        "x": L0_attn_x, "wqkvT": np.transpose(L0_attn_qkv_w), "bqkv": np.reshape(L0_attn_qkv_b, (1, -1)),
        "wprojT": np.transpose(L0_attn_proj_w), "bproj": np.reshape(L0_attn_proj_b, (1, -1)),
        "w_router": L0_ffn_W_router, "w_up": L0_ffn_W_up, "w_down": L0_ffn_W_down,
        "w_sup": L0_ffn_W_sh_up, "w_sdown": L0_ffn_W_sh_down,
    }
    arrays = {f"in_{k}": np.ascontiguousarray(v) for k, v in given.items()}
    args = [nc.dram_tensor(n, a.shape, F32, kind="ExternalInput").ap() for n, a in arrays.items()]
    out = nc.dram_tensor("out_0", (B, T, D), F32, kind="ExternalOutput").ap()
    slots = nc.dram_tensor("slots", (NT * P, D), F32, kind="Internal").ap()
    results = nc.dram_tensor("results", (NT * P, D), F32, kind="Internal").ap()
    build(nc, *args, slots, results, out)
    return run_bass_kernel_spmd(nc, [arrays], core_ids=[0]).results[0]["out_0"]
```
